# Optimizing a Trainium2 kernel written in Bass

```python
import numpy as np
import jax
import jax.numpy as jnp

def _softmax(x, axis=-1):
    return jax.nn.softmax(x, axis=axis)

def _gelu(x):
    return jax.nn.gelu(x, approximate=True)

def _silu(x):
    return jax.nn.silu(x)

def _sigmoid(x):
    return jax.nn.sigmoid(x)

def _layernorm(x, axis=-1, eps=1e-05):
    m = jnp.mean(x, axis=axis, keepdims=True)
    v = jnp.var(x, axis=axis, keepdims=True)
    return (x - m) / jnp.sqrt(v + eps)

def _scatter_add(tgt, idx, src, axis=0):
    return tgt.at[idx].add(src)

def _segment_sum(src, seg, n):
    return jax.ops.segment_sum(src, seg, n)
kernel_name = 'mk_gnn_preln_d4_gnn_r8_32f4c2'

def setup_inputs(seed: int=0):
    np.random.seed(seed)
    _w = jnp.asarray

    def _rec_inputs():
        import jax
        import jax.numpy as jnp
        _gk = jax.random.key(seed)
        x = -0.0005121 + 1.001 * jax.random.normal(jax.random.fold_in(_gk, 1), (12500, 64), jnp.float32)
        _s = jax.random.randint(jax.random.fold_in(_gk, 2), (100000,), 0, 12500, jnp.int32)
        _d = jax.random.randint(jax.random.fold_in(_gk, 3), (100000,), 0, 12500, jnp.int32)
        _loop = jnp.arange(12500, dtype=jnp.int32)
        src = jnp.concatenate([_s, _d, _loop])
        dst = jnp.concatenate([_d, _s, _loop])
        _o = jnp.argsort(dst, stable=True)
        src = src[_o]
        dst = dst[_o]
        edge_attr_3 = 0.00117183 + 1.0004 * jax.random.normal(jax.random.fold_in(_gk, 12), (212500, 3), jnp.float32)
        edge_weight = jax.random.uniform(jax.random.fold_in(_gk, 14), (212500,), jnp.float32, 0.0, 0.999999)
        return (x, src, dst, edge_attr_3, edge_weight)
    x, src, dst, edge_attr_3, edge_weight = _rec_inputs()

    def _L0_gnn_setup():
        import jax, jax.numpy as jnp
        import numpy as np
        N_NODES = 6250
        N_EDGES = 125000
        D = 64
        L = 3
        BN_EPS = 1e-05
        key = jax.random.key(seed)
        ks = jax.random.split(key, 6)
        x = jax.random.normal(ks[0], (N_NODES, D), dtype=jnp.float32)
        edge_src = jax.random.randint(ks[1], (N_EDGES,), 0, N_NODES)
        edge_dst = jax.random.randint(ks[2], (N_EDGES,), 0, N_NODES)
        edge_weight = jax.random.uniform(ks[3], (N_EDGES,), dtype=jnp.float32)
        W = jax.random.normal(ks[4], (L, D, D), dtype=jnp.float32) * (1.0 / np.sqrt(D))
        b = jnp.zeros((L, D), dtype=jnp.float32)
        prelu_a = jnp.full((L,), 0.25, dtype=jnp.float32)
        bn_gamma = jnp.ones((L, D), dtype=jnp.float32)
        bn_beta = jnp.zeros((L, D), dtype=jnp.float32)
        return {'x': x, 'edge_src': edge_src, 'edge_dst': edge_dst, 'edge_weight': edge_weight, 'W': W, 'b': b, 'prelu_a': prelu_a, 'bn_gamma': bn_gamma, 'bn_beta': bn_beta}
    _L0_gnn_all = _L0_gnn_setup()
    _L0_gnn_in = {k: v for k, v in _L0_gnn_all.items() if k in ('W', 'b', 'prelu_a', 'bn_gamma', 'bn_beta')}
    del _L0_gnn_all

    def _L1_gnn_setup():
        import jax, jax.numpy as jnp
        import numpy as np
        N = 12500
        E = 200000
        IN, HID, OUT = (64, 128, 64)
        key = jax.random.key(seed)
        ks = jax.random.split(key, 9)
        x = jax.random.normal(ks[0], (N, IN), dtype=jnp.float32)
        edge_index = jax.random.randint(ks[1], (2, E), 0, N, dtype=jnp.int32)
        edge_weight = jax.random.uniform(ks[2], (E,), dtype=jnp.float32)
        W1 = jax.random.normal(ks[3], (HID, IN), jnp.float32) * (1.0 / np.sqrt(IN))
        b1 = jnp.zeros((HID,), jnp.float32)
        W2 = jax.random.normal(ks[4], (HID, HID), jnp.float32) * (1.0 / np.sqrt(HID))
        b2 = jnp.zeros((HID,), jnp.float32)
        W3 = jax.random.normal(ks[5], (OUT, HID), jnp.float32) * (1.0 / np.sqrt(HID))
        b3 = jnp.zeros((OUT,), jnp.float32)
        return {'x': x, 'edge_index': edge_index, 'edge_weight': edge_weight, 'W1': W1, 'b1': b1, 'W2': W2, 'b2': b2, 'W3': W3, 'b3': b3}
    _L1_gnn_all = _L1_gnn_setup()
    _L1_gnn_in = {k: v for k, v in _L1_gnn_all.items() if k in ('W1', 'b1', 'W2', 'b2', 'W3', 'b3')}
    del _L1_gnn_all

    def _L2_gnn_setup():
        import jax, jax.numpy as jnp
        import numpy as np
        N_NODES = 12500
        key = jax.random.key(seed)
        k1, k2, k3 = jax.random.split(key, 3)
        feat = jax.random.normal(k1, (N_NODES, 64), dtype=jnp.float32)
        src = jax.random.randint(k2, (156250,), 0, N_NODES, dtype=jnp.int64)
        dst = jax.random.randint(k3, (156250,), 0, N_NODES, dtype=jnp.int64)
        return {'feat': feat, 'src': src, 'dst': dst}
    _L2_gnn_all = _L2_gnn_setup()
    _L2_gnn_in = {k: v for k, v in _L2_gnn_all.items() if k in ()}
    del _L2_gnn_all

    def _L3_gnn_setup():
        import jax, jax.numpy as jnp
        import numpy as np
        M = 6250
        E = 100000
        C_IN = 64
        C_OUT = 64
        DIM = 3
        RADIUS = 1.0
        EPS = 1e-05

        def layer_norm(x, g, b):
            mu = jnp.mean(x, axis=-1, keepdims=True)
            var = jnp.mean((x - mu) ** 2, axis=-1, keepdims=True)
            return (x - mu) * jax.lax.rsqrt(var + EPS) * g + b
        key = jax.random.key(seed)
        ks = jax.random.split(key, 12)
        inv = 1.0 / np.sqrt(C_OUT)
        return {'source': jax.random.randint(ks[0], (E,), 0, M), 'target': jax.random.randint(ks[1], (E,), 0, M), 'features': jax.random.normal(ks[2], (M, C_IN), dtype=jnp.float32), 'hood_coords': jax.random.normal(ks[3], (E, DIM), dtype=jnp.float32), 'Wd1': jax.random.normal(ks[4], (DIM, C_OUT), dtype=jnp.float32) / np.sqrt(DIM), 'bd1': jnp.zeros((C_OUT,), jnp.float32), 'g1': jnp.ones((C_OUT,), jnp.float32), 'b1': jnp.zeros((C_OUT,), jnp.float32), 'Wd2': jax.random.normal(ks[5], (C_OUT, C_OUT), dtype=jnp.float32) * inv, 'bd2': jnp.zeros((C_OUT,), jnp.float32), 'g2': jnp.ones((C_OUT,), jnp.float32), 'b2': jnp.zeros((C_OUT,), jnp.float32), 'W1': jax.random.normal(ks[6], (C_IN, C_OUT), dtype=jnp.float32) / np.sqrt(C_IN), 'W2': jax.random.normal(ks[7], (C_IN, C_OUT), dtype=jnp.float32) / np.sqrt(C_IN), 'W3': jax.random.normal(ks[8], (C_IN, C_OUT), dtype=jnp.float32) / np.sqrt(C_IN)}
    _L3_gnn_all = _L3_gnn_setup()
    _L3_gnn_in = {k: v for k, v in _L3_gnn_all.items() if k in ('Wd1', 'bd1', 'g1', 'b1', 'Wd2', 'bd2', 'g2', 'b2', 'W1', 'W2', 'W3')}
    del _L3_gnn_all
    return {'x': x, 'src': src, 'dst': dst, 'edge_attr_3': edge_attr_3, 'edge_weight': edge_weight, 'L0_gnn_W': _L0_gnn_in['W'], 'L0_gnn_b': _L0_gnn_in['b'], 'L0_gnn_prelu_a': _L0_gnn_in['prelu_a'], 'L0_gnn_bn_gamma': _L0_gnn_in['bn_gamma'], 'L0_gnn_bn_beta': _L0_gnn_in['bn_beta'], 'L1_gnn_W1': _L1_gnn_in['W1'], 'L1_gnn_b1': _L1_gnn_in['b1'], 'L1_gnn_W2': _L1_gnn_in['W2'], 'L1_gnn_b2': _L1_gnn_in['b2'], 'L1_gnn_W3': _L1_gnn_in['W3'], 'L1_gnn_b3': _L1_gnn_in['b3'], 'L3_gnn_Wd1': _L3_gnn_in['Wd1'], 'L3_gnn_bd1': _L3_gnn_in['bd1'], 'L3_gnn_g1': _L3_gnn_in['g1'], 'L3_gnn_b1': _L3_gnn_in['b1'], 'L3_gnn_Wd2': _L3_gnn_in['Wd2'], 'L3_gnn_bd2': _L3_gnn_in['bd2'], 'L3_gnn_g2': _L3_gnn_in['g2'], 'L3_gnn_b2': _L3_gnn_in['b2'], 'L3_gnn_W1': _L3_gnn_in['W1'], 'L3_gnn_W2': _L3_gnn_in['W2'], 'L3_gnn_W3': _L3_gnn_in['W3']}

def reference(x, src, dst, edge_attr_3, edge_weight, L0_gnn_W, L0_gnn_b, L0_gnn_prelu_a, L0_gnn_bn_gamma, L0_gnn_bn_beta, L1_gnn_W1, L1_gnn_b1, L1_gnn_W2, L1_gnn_b2, L1_gnn_W3, L1_gnn_b3, L3_gnn_Wd1, L3_gnn_bd1, L3_gnn_g1, L3_gnn_b1, L3_gnn_Wd2, L3_gnn_bd2, L3_gnn_g2, L3_gnn_b2, L3_gnn_W1, L3_gnn_W2, L3_gnn_W3):
    import jax
    import jax.numpy as jnp

    def _L0_gnn_ref(x, edge_src, edge_dst, edge_weight, W, b, prelu_a, bn_gamma, bn_beta):
        import jax, jax.numpy as jnp
        import numpy as np
        N_NODES = 6250
        N_EDGES = 125000
        D = 64
        L = 3
        BN_EPS = 1e-05
        n = x.shape[0]
        h = x
        for i in range(L):
            h_in = h
            xw = h @ W[i]
            msg = edge_weight[:, None] * xw[edge_src]
            agg = jax.ops.segment_sum(msg, edge_dst, num_segments=n) + b[i]
            h = jnp.where(agg >= 0, agg, prelu_a[i] * agg)
            if i > 0:
                h = h + h_in
            mean = jnp.mean(h, axis=0)
            var = jnp.mean((h - mean) ** 2, axis=0)
            h = bn_gamma[i] * (h - mean) * jax.lax.rsqrt(var + BN_EPS) + bn_beta[i]
        return h

    def _L1_gnn_ref(x, edge_index, edge_weight, W1, b1, W2, b2, W3, b3):
        import jax, jax.numpy as jnp
        import numpy as np
        N = 12500
        E = 200000
        IN, HID, OUT = (64, 128, 64)
        n = x.shape[0]
        loop = jnp.arange(n, dtype=edge_index.dtype)
        src = jnp.concatenate([edge_index[0], loop])
        dst = jnp.concatenate([edge_index[1], loop])
        ew = jnp.concatenate([edge_weight, jnp.ones((n,), x.dtype)])
        deg = jax.ops.segment_sum(jnp.ones_like(ew), src, num_segments=n)
        dinv = jax.lax.rsqrt(deg)
        norm = dinv[src] * ew * dinv[dst]

        def layer(h, W, b):
            m = h @ W.T + b
            agg = jax.ops.segment_sum(norm[:, None] * m[src], dst, num_segments=n)
            return jax.nn.relu(agg)
        h = layer(x, W1, b1)
        h = layer(h, W2, b2)
        return layer(h, W3, b3)

    def _L2_gnn_ref(feat, src, dst):
        import jax, jax.numpy as jnp
        import numpy as np
        N_NODES = 12500
        n = feat.shape[0]
        ones = jnp.ones(src.shape[0], dtype=feat.dtype)
        out_deg = jax.ops.segment_sum(ones, src, num_segments=n)
        in_deg = jax.ops.segment_sum(ones, dst, num_segments=n)
        norm_l = jax.lax.rsqrt(jnp.maximum(out_deg, 1.0) + 1.0)
        norm_r = jax.lax.rsqrt(jnp.maximum(in_deg, 1.0) + 1.0)
        feat_src = feat * norm_l[:, None]
        msgs = feat_src[src]
        h_neigh = jax.ops.segment_sum(msgs, dst, num_segments=n)
        rst = (feat + h_neigh) * norm_r[:, None]
        return rst

    def _L3_gnn_ref(source, target, features, hood_coords, Wd1, bd1, g1, b1, Wd2, bd2, g2, b2, W1, W2, W3):
        import jax, jax.numpy as jnp
        import numpy as np
        M = 6250
        E = 100000
        C_IN = 64
        C_OUT = 64
        DIM = 3
        RADIUS = 1.0
        EPS = 1e-05

        def layer_norm(x, g, b):
            mu = jnp.mean(x, axis=-1, keepdims=True)
            var = jnp.mean((x - mu) ** 2, axis=-1, keepdims=True)
            return (x - mu) * jax.lax.rsqrt(var + EPS) * g + b
        m = features.shape[0]
        x = hood_coords / RADIUS
        d = jax.nn.gelu(layer_norm(x @ Wd1 + bd1, g1, b1), approximate=False)
        d = jax.nn.gelu(layer_norm(d @ Wd2 + bd2, g2, b2), approximate=False)
        w1 = features @ W1
        w2 = features @ W2
        w3 = features @ W3
        logits = w1[target] - w2[source] + d
        seg_max = jax.ops.segment_max(logits, target, num_segments=m)
        seg_max = jnp.where(jnp.isfinite(seg_max), seg_max, 0.0)
        e = jnp.exp(logits - seg_max[target])
        denom = jax.ops.segment_sum(e, target, num_segments=m)
        a = e / denom[target]
        out = jax.ops.segment_sum(a * (w3[source] + d), target, num_segments=m)
        return out
    edge_index = jnp.stack([src, dst])
    h = jnp.maximum(_layernorm(x, axis=-1), 0.0)
    x = x + _L0_gnn_ref(h, src, dst, edge_weight, L0_gnn_W, L0_gnn_b, L0_gnn_prelu_a, L0_gnn_bn_gamma, L0_gnn_bn_beta)
    h = jnp.maximum(_layernorm(x, axis=-1), 0.0)
    x = x + _L1_gnn_ref(h, edge_index, edge_weight, L1_gnn_W1, L1_gnn_b1, L1_gnn_W2, L1_gnn_b2, L1_gnn_W3, L1_gnn_b3)
    h = jnp.maximum(_layernorm(x, axis=-1), 0.0)
    x = x + _L2_gnn_ref(h, src, dst)
    h = jnp.maximum(_layernorm(x, axis=-1), 0.0)
    x = x + _L3_gnn_ref(src, dst, h, edge_attr_3, L3_gnn_Wd1, L3_gnn_bd1, L3_gnn_g1, L3_gnn_b1, L3_gnn_Wd2, L3_gnn_bd2, L3_gnn_g2, L3_gnn_b2, L3_gnn_W1, L3_gnn_W2, L3_gnn_W3)
    return x

_drawn_inputs = setup_inputs


def setup_inputs(seed=0):
    import zlib

    import numpy as np

    out = dict(_drawn_inputs(seed))
    spreads = {'L0_gnn_b': (0.0, 1.297),
     'L0_gnn_prelu_a': (0.25, 0.6),
     'L0_gnn_bn_gamma': (1.0, 0.2),
     'L0_gnn_bn_beta': (0.0, 0.1),
     'L1_gnn_b1': (0.0, 0.8),
     'L1_gnn_b2': (0.0, 0.757),
     'L1_gnn_b3': (0.0, 0.293),
     'L3_gnn_bd1': (0.0, 0.384),
     'L3_gnn_g1': (1.0, 0.6),
     'L3_gnn_b1': (0.0, 0.577),
     'L3_gnn_bd2': (0.0, 0.31),
     'L3_gnn_g2': (1.0, 0.2),
     'L3_gnn_b2': (0.0, 0.545)}
    factors = {'L1_gnn_W1': 7.515,
     'L1_gnn_W2': 6.475,
     'L1_gnn_W3': 4.346,
     'L3_gnn_W1': 200.0,
     'L3_gnn_W2': 6.506}
    for name, (base, spread) in spreads.items():
        noise = np.random.default_rng([zlib.crc32(name.encode()), seed]).standard_normal(out[name].shape)
        drawn = base * np.exp(spread * noise) if base else spread * noise
        out[name] = jnp.asarray(drawn.astype(out[name].dtype))
    for name, factor in factors.items():
        out[name] = (out[name] * factor).astype(out[name].dtype)
    return out
```

```python
from concourse import mybir
import concourse.bass as bass
from concourse.alu_op_type import AluOpType as ALU

N_NODES = 12500
N_EDGES = 212500
D = 64
P = 128
BLOCKS = -(-N_NODES // P)
NP = BLOCKS * P
NW = NP + P
K = 16
TURNS = -(-N_EDGES // (K * P))
CHUNKS = TURNS * K
EDGES = CHUNKS * P
HALF = EDGES // 2
GROUP = 8
GCOLS = GROUP // 2 * P
GROUPS = CHUNKS // GROUP
PASSES = 8
SB = 7
STEPS = BLOCKS // SB
SC = SB * P
BN_CHUNK = 500
BN_PART = 2500
EPS = 1e-5
BIG = 1e30
assert BLOCKS == STEPS * SB and STEPS % 2 == 0 and N_NODES % BN_PART == 0 and N_EDGES < EDGES

F32 = mybir.dt.float32
BF16 = mybir.dt.bfloat16
I32 = mybir.dt.int32
ACT = mybir.ActivationFunctionType
AX = mybir.AxisListType

STAGES = [
    ("L0 layer 0 table", "norm", 64, 64, "table"),
    ("L0 layer 1 table", "affine", 64, 64, "table"),
    ("L0 layer 2 table", "affine", 64, 64, "table"),
    ("L0 residual", "affine", 64, 64, "add"),
    ("L1 layer 1 table", "norm", 64, 128, "gcn_first"),
    ("L1 layer 2 table", "relu", 128, 128, "gcn"),
    ("L1 layer 3 table", "relu", 128, 64, "gcn"),
    ("L1 residual", "relu", 64, 64, "add_dinv"),
    ("L2 table", "norm_only", 64, 64, "scaled"),
    ("L2 residual", "copy", 64, 64, "add_norm_r"),
    ("L3 tables", "norm", 64, 128, "attention"),
    ("L3 residual", "copy", 128, 128, "add_ratio"),
]
TABLE_STAGES = [n for n, s in enumerate(STAGES) if not s[4].startswith("add")]
NORM_STAGES = [n for n, s in enumerate(STAGES) if s[1].startswith("norm")]
INIT_STAGES = [n for n, s in enumerate(STAGES) if s[4].startswith("gcn")]
ZERO_STAGES = [0, 1, 2, 10]
PASS_AFTER = {0: 0, 1: 1, 2: 2, 4: 3, 5: 4, 6: 5, 8: 6, 10: 7}
PASS_WIDTH = [64, 64, 64, 128, 128, 64, 64, 128]


def turns(eng, n, peel=1):
    for t in range(min(peel, n)):
        yield t
    if n > peel:
        with eng.Fori(peel, n) as t:
            yield t


class Own:

    def __init__(self, eng, sem):
        self.eng, self.sem, self.base, self.off = eng, sem, 0, 0

    def step(self, ins):
        ins.then_inc(self.sem, 1)
        self.base += 1
        return self.base

    def wait(self, value=None):
        self.eng.wait_ge(self.sem, (self.base if value is None else value) + self.off)

    def link(self, ins):
        self.step(ins)
        self.wait()

    def turns(self, n, each, peel=1):
        for t in range(min(peel, n)):
            yield t
        if n > peel:
            start = self.base
            with self.eng.Fori(peel, n) as t:
                self.off = (t - peel) * each
                yield t
                assert self.base == start + each, (self.base - start, each)
            self.off = 0
            self.base = start + each * (n - peel)


def build(nc, a):
    from contextlib import ExitStack

    ctx = ExitStack()
    with ctx:
        def sb(name, shape, dt=F32):
            return ctx.enter_context(nc.sbuf_tensor(name, shape, dt))

        def sem(name):
            return ctx.enter_context(nc.semaphore(name))

        def dram(name, shape, dt=F32):
            return nc.dram_tensor(name, shape, dt).ap()

        table64 = dram("table64", [NP, 64])
        table128 = dram("table128", [NP, 128])
        w1_table = dram("w1_table", [NW, 64])
        edge_d = dram("edge_d", [P, HALF])

        agg = sb("agg", [P, NW])
        wide = sb("wide", [P, NP])
        xn = sb("xn", [P, BLOCKS, D])
        src_i = sb("src_i", [P, CHUNKS + K], I32)
        dst_i = sb("dst_i", [P, CHUNKS], I32)
        dst_l = sb("dst_l", [P, CHUNKS])
        weight = sb("weight", [P, CHUNKS])
        base = sb("base", [1, CHUNKS], I32)
        ring = sb("ring", [P, 2560])
        stage = sb("stage", [P, 2, SB * 192])
        idx = sb("idx", [P, K], I32)
        ident = sb("ident", [P, P])
        neg_ident = sb("neg_ident", [P, P])
        iota = sb("iota", [P, P])
        iota_p = sb("iota_p", [P, 1])
        l0_w = sb("l0_w", [D, 3, D])
        l0_b = sb("l0_b", [D, 3])
        l0_gamma = sb("l0_gamma", [D, 3])
        l0_beta = sb("l0_beta", [D, 3])
        l0_prelu = sb("l0_prelu", [D, 3])
        l1_w1 = sb("l1_w1", [D, 128])
        l1_w2 = sb("l1_w2", [P, 128])
        l1_w3 = sb("l1_w3", [P, 64])
        l1_b = sb("l1_b", [P, 320])
        l3_w = sb("l3_w", [D, 192])
        mlp = sb("mlp", [P, 2, 128])
        mlp_d = sb("mlp_d", [P, 2, 64])
        mlp_b = sb("mlp_b", [P, 2, 3])
        centred = sb("centred", [P, 2])
        small = sb("small", [P, 16])
        stats = sb("stats", [D, N_NODES // BN_CHUNK, 6])
        bn = sb("bn", [D, 8])
        ln = sb("ln", [P, 4, BLOCKS])
        deg = sb("deg", [P, 3, BLOCKS])
        zeros_b = sb("zeros_b", [P, P], BF16)
        blk = sb("blk", [P, P])
        hist_i = sb("hist_i", [P, 2, K], I32)
        end_a = sb("end_a", [P, 1], I32)

        gathered = ring[:, 0:K * P].rearrange("p (k w) -> p k w", k=K)
        onehot = ring[:, K * P:2560].rearrange("p (k w) -> p k w", k=4)
        zbuf = ring[:, 0:2 * SC].rearrange("p (h c) -> p h c", h=2)
        prelu_neg = ring[0:D, 0:BN_PART]
        prelu_pos = stage[0:D].rearrange("p h c -> p (h c)")[:, 0:BN_PART]
        hist_lo = stage[:, 0, 0:1024].bitcast(BF16).rearrange("p (k w) -> p k w", k=K)
        hist_hi = stage[:, 1, 0:K * BLOCKS // 2].bitcast(BF16).rearrange("p (k w) -> p k w", k=K)

        hn = wide[:, 0:BLOCKS * D].rearrange("p (b d) -> p b d", d=D)
        sq = wide[:, BLOCKS * D:2 * BLOCKS * D].rearrange("p (b d) -> p b d", d=D)
        hblk = wide[:, BLOCKS * D:BLOCKS * D + 2 * SB * D].rearrange("p (h b d) -> p h b d", h=2, d=D)
        h_in = wide[0:D, :]
        TC = K // 2 * P
        e_in = wide[0:6, 0:2 * TC].rearrange("p (h c) -> p h c", h=2)
        e_sq = wide[:, 2 * TC:3 * TC]
        e_sd = wide[:, 3 * TC:4 * TC]
        e_y = wide[:, 4 * TC:5 * TC]
        e_z = wide[:, 5 * TC:6 * TC]
        e_out = wide[:, 6 * TC:8 * TC].rearrange("p (h c) -> p h c", h=2)
        at = [0]

        def part(n):
            at[0] += n
            return wide[:, at[0] - n:at[0]]

        dt_in = part(2 * GCOLS).rearrange("p (h c) -> p h c", h=2)
        dst_ab = part(4 * GCOLS).bitcast(I32).rearrange("p (h s c) -> p h s c", h=2, s=2)
        dst_pair = part(2 * (GCOLS + 2)).bitcast(I32).rearrange("p (h c) -> p h c", h=2)
        w1_win = part(K * 64).rearrange("p (k w) -> p k w", k=K)
        spread = part(GROUP * P).rearrange("p (k w) -> p k w", k=GROUP)
        scaled = part(GCOLS + 2)
        rr = part(GCOLS)
        pp = part(GCOLS)
        pw = part(GCOLS)
        mm = part(2 * (GCOLS + 2)).rearrange("p (h c) -> p h c", h=2)
        oo = part(2 * GCOLS).rearrange("p (h c) -> p h c", h=2)
        ss = part(2 * GCOLS).rearrange("p (h c) -> p h c", h=2)
        assert at[0] <= NP, at[0]
        sflat = stage[:].rearrange("p h c -> p (h c)")
        os_rows = sflat[:, 0:GROUP * P].rearrange("p (j s w) -> p j s w", j=4, s=2)
        m_rows = sflat[:, 1024:1280].rearrange("p (j w) -> p j w", j=4)
        next_i = sflat[:, 0:CHUNKS].bitcast(I32)
        star_sel = sflat[:, CHUNKS:CHUNKS + CHUNKS // 2]
        fix = sflat[:, 2560:2576]

        zero = small[:, 6:7]

        psum = ctx.enter_context(nc.psum_tensor("psum", [P, 8, 512], F32))
        flat = psum.rearrange("p b c -> p (b c)")
        prod = [flat[:, 1024 * h:1024 * h + SC] for h in range(2)]
        prod_w1 = [psum[:, 4 + h, 0:SB * 64] for h in range(2)]
        back = flat[:, 2048:2048 + SC]
        turned = flat[:, 3072:3072 + SC]
        window = [psum[:, 4 + k, 0:P] for k in range(4)]
        window3 = [psum[:, 5 + k, 0:P] for k in range(2)]
        hist = psum[:, 0, 0:BLOCKS]
        e_prod = flat[:, 0:TC]
        e_var = flat[:, 1024:1024 + TC]
        logit = [psum[:, 0, :], psum[:, 1, :]]
        value = psum[:, 2, :]
        o_back, s_back, m_back = psum[:, 3, :], psum[:, 4, :], psum[:, 3, :]
        star = psum[0:D, 7, 0:1]
        setup_ps = psum[:, 0, 0:8]
        fix_ps = psum[:, 3, 0:4]

        loaded = sem("loaded")
        rows_loaded = sem("rows_loaded")
        pads_done = sem("pads_done")
        moved = sem("moved")
        consts = sem("consts")
        pool_own = sem("pool_own")
        dve_own = sem("dve_own")
        act_own = sem("act_own")
        dve_setup = sem("dve_setup")
        pe_setup = sem("pe_setup")
        ln_var = sem("ln_var")
        ln_sd = sem("ln_sd")
        h_ready = sem("h_ready")
        h_turned = sem("h_turned")
        z_ready = sem("z_ready")
        z_used = sem("z_used")
        finished = sem("finished")
        stored = [sem("stored0"), sem("stored1")]
        w1_stored = [sem("w1_stored0"), sem("w1_stored1")]
        back_ready = sem("back_ready")
        init_done = sem("init_done")
        zero_done = sem("zero_done")
        idx_ready = sem("idx_ready")
        gathered_s = [sem(f"gathered{k}") for k in range(K)]
        onehot_ready = sem("onehot_ready")
        summed = sem("summed")
        added = sem("added")
        relu_done = sem("relu_done")
        prelu_done = sem("prelu_done")
        dve_stats = sem("dve_stats")
        bn_var = sem("bn_var")
        bn_sd = sem("bn_sd")
        bn_done = sem("bn_done")
        e_loaded = [sem("e_loaded0"), sem("e_loaded1")]
        e_mm = sem("e_mm")
        e_act = sem("e_act")
        e_dve = sem("e_dve")
        e_stored = [sem("e_stored0"), sem("e_stored1")]
        hist_ready = sem("hist_ready")
        hist_used = sem("hist_used")
        hist_closed = sem("hist_closed")
        deg_sum = sem("deg_sum")
        deg_sd = sem("deg_sd")
        in3 = [sem("in3_0"), sem("in3_1")]
        star_ready = sem("star_ready")
        spread_ready = sem("spread_ready")
        logits_ready = sem("logits_ready")
        values_ready = sem("values_ready")
        scaled_ready = sem("scaled_ready")
        shift_ready = sem("shift_ready")
        excess_ready = sem("excess_ready")
        factor_ready = sem("factor_ready")
        p_ready = sem("p_ready")
        scans_done = sem("scans_done")
        turned_back = sem("turned_back")
        o_copied = sem("o_copied")
        m_turned = sem("m_turned")
        rows_ready = sem("rows_ready")
        pw_ready = sem("pw_ready")
        next_loaded = sem("next_loaded")
        fix_dve = sem("fix_dve")
        fix_pe = sem("fix_pe")
        fix_act = sem("fix_act")
        out_ready = sem("out_ready")
        out_stored = sem("out_stored")

        N_LOADS = 22
        IN3 = GROUP + 5
        PASS0 = lambda q: q * CHUNKS
        TURN0 = lambda q: q * TURNS

        passed = {}

        def settle(eng):
            if eng not in passed:
                passed[eng] = sem(f"passed{len(passed)}")
            eng.sem_inc(passed[eng], 1)

        def stored_at(f):
            return sum(1 for n in TABLE_STAGES if n < f) * (STEPS // 2)

        block = ctx.enter_context(nc.Block())

        @block.sync
        def _(sp):
            sp.dma_start(xn[:], a["x"].rearrange("(b p) d -> p b d", p=P)).then_inc(loaded, 16)
            small_loads = [
                (l0_w[:], a["l0_w"].rearrange("l i o -> i l o")),
                (l0_b[:], a["l0_b"]), (l0_gamma[:], a["l0_gamma"]), (l0_beta[:], a["l0_beta"]),
                (l0_prelu[:], a["l0_prelu"].partition_broadcast(D)),
                (l1_w1[:], a["l1_w1"]), (l1_w2[:], a["l1_w2"]), (l1_w3[:], a["l1_w3"]),
                (l1_b[:], a["l1_b"].partition_broadcast(P)),
                (l3_w[:, 0:64], a["l3_w2"]), (l3_w[:, 64:128], a["l3_w3"]), (l3_w[:, 128:192], a["l3_w1"]),
                (mlp_d[0:3, 0, :], a["wd1"]), (mlp_d[3:6, 0, :], a["wd1"]),
                (mlp_d[0:D, 1, :], a["wd2"]), (mlp_d[D:P, 1, :], a["wd2"]),
                (mlp_b[0:D, 0, :], a["mlp_b"][:, 0, :]), (mlp_b[D:P, 0, :], a["mlp_b"][:, 0, :]),
                (mlp_b[0:D, 1, :], a["mlp_b"][:, 1, :]), (mlp_b[D:P, 1, :], a["mlp_b"][:, 1, :]),
                (end_a[:], a["dst_rows"][0:1, HALF:HALF + 1].partition_broadcast(P).rearrange("p a c -> p (a c)")),
            ]
            for to, of in small_loads:
                sp.dma_start(to, of).then_inc(loaded, 16)
            sp.dma_start(src_i[:], a["src"]).then_inc(rows_loaded, 16)
            sp.dma_start(dst_i[:], a["dst"]).then_inc(rows_loaded, 16)
            sp.dma_start(weight[:], a["ew"]).then_inc(rows_loaded, 16)
            sp.dma_start(base[:], a["base"]).then_inc(rows_loaded, 16)
            sp.dma_start(agg[:, 0:CHUNKS].bitcast(I32), a["base"].partition_broadcast(P).rearrange("p a c -> p (a c)"))\
                .then_inc(rows_loaded, 16)
            assert len(small_loads) + 1 == N_LOADS
            sp.wait_ge(dve_setup, 1)
            sp.dma_start(mlp[0:3, 0, 0:64], mlp_d[0:3, 0, :]).then_inc(moved, 16)
            sp.dma_start(mlp[3:6, 0, 64:128], mlp_d[3:6, 0, :]).then_inc(moved, 16)
            sp.wait_ge(consts, 4)
            sp.dma_start(w1_table[NP:NW, :], neg_ident[:, 0:64]).then_inc(pads_done, 16)

            def store_tables(f):
                name, source, wi, wo, finish = STAGES[f]
                table = (table128 if wo == 128 else table64).rearrange("(i b p) w -> i p b w", b=SB, p=P)
                w1 = w1_table[0:NP, :].rearrange("(i b p) w -> i p b w", b=SB, p=P)
                with sp.Fori(0, STEPS // 2) as j:
                    for h in range(2):
                        i = 2 * j + h
                        sp.wait_ge(finished, f * STEPS + i + 1)
                        rows = stage[:, h, :]
                        sp.dma_start(table[bass.ds(i, 1)].rearrange("o p b w -> (o p) b w"),
                                     rows[:, 0:SB * wo].rearrange("p (b w) -> p b w", b=SB)).then_inc(stored[h], 16)
                        if finish == "attention":
                            sp.dma_start(w1[bass.ds(i, 1)].rearrange("o p b w -> (o p) b w"),
                                         rows[:, SB * 128:SB * 192].rearrange("p (b w) -> p b w", b=SB))\
                                .then_inc(w1_stored[h], 16)

            store_tables(0)

            def edge_load(j, h):
                sp.dma_start(e_in[:, h, :], a["edge_attr"][:, bass.ds((2 * j + h) * TC, TC)]).then_inc(e_loaded[h], 16)

            def edge_store(t, h):
                sp.wait_ge(e_act, 6 * t + 6)
                sp.dma_start(edge_d[:, bass.ds(t * TC, TC)], e_out[:, h, :]).then_inc(e_stored[h], 16)

            edge_load(0, 0)
            edge_load(0, 1)
            with sp.Fori(0, TURNS // 2 - 1) as j:
                for h in range(2):
                    sp.wait_ge(e_mm, 4 * (2 * j + h) + 1)
                    edge_load(j + 1, h)
                    edge_store(2 * j + h, h)
            for h in range(2):
                edge_store(TURNS - 2 + h, h)
            for h in range(2):
                sp.wait_ge(e_stored[h], 16 * (TURNS // 2))

            for f in TABLE_STAGES[1:]:
                store_tables(f)

            for h in range(2):
                sp.wait_ge(stored[h], 16 * stored_at(12))
                sp.wait_ge(w1_stored[h], 16 * (STEPS // 2))
            sp.dma_start(next_i, a["dst_next"]).then_inc(next_loaded, 16)
            sp.wait_ge(pads_done, 16)
            sp.wait_ge(zero_done, len(ZERO_STAGES) * STEPS + 1)

            def attention_loads(c, h):
                begin = nc.values_load_multi_w_load_instructions(
                    base[0:1, bass.ds(c * GROUP, GROUP)], engines=[mybir.EngineType.SP], min_val=0, max_val=N_NODES,
                    skip_runtime_bounds_check_because="destinations are nodes")[1]
                for k in range(GROUP):
                    sp.dma_start(w1_win[:, h * GROUP + k, :], w1_table[bass.ds(begin[k], P), :]).then_inc(in3[h], 16)
                sp.dma_start(dt_in[:, h, :], edge_d[:, bass.ds(c * GCOLS, GCOLS)]).then_inc(in3[h], 16)
                for s in range(2):
                    sp.dma_start(dst_ab[:, h, s, :],
                                 a["dst_rows"][s:s + 1, bass.ds(c * GCOLS + 1, GCOLS)].partition_broadcast(P)
                                 .rearrange("p a c -> p (a c)")).then_inc(in3[h], 16)
                    sp.dma_start(dst_pair[s * D:(s + 1) * D, h, 0:GCOLS + 1],
                                 a["dst_rows"][s:s + 1, bass.ds(c * GCOLS, GCOLS + 1)].partition_broadcast(D)
                                 .rearrange("p a c -> p (a c)")).then_inc(in3[h], 16)

            for t in turns(sp, TURNS):
                for h in range(2):
                    c = 2 * t + h
                    if not (isinstance(t, int) and t == 0):
                        sp.wait_ge(spread_ready, (c - 1) * GROUP)
                        sp.wait_ge(values_ready, c - 1)
                        sp.wait_ge(scaled_ready, c - 1)
                    attention_loads(c, h)

            sp.wait_ge(out_ready, 1)
            full = N_NODES // P
            sp.dma_start(a["out"][0:full * P, :].rearrange("(b p) d -> p b d", p=P), xn[:, 0:full, :])\
                .then_inc(out_stored, 16)
            sp.dma_start(a["out"][full * P:N_NODES, :], xn[0:N_NODES - full * P, full, :]).then_inc(out_stored, 16)
            sp.wait_ge(out_stored, 32)

        @block.gpsimd
        def _(pool):
            own = Own(pool, pool_own)
            pool.iota(iota[:], [[1, P]], base=0, channel_multiplier=0,
                      allow_small_or_imprecise_dtypes=True).then_inc(consts, 1)
            pool.iota(iota_p[:], [[0, 1]], base=0, channel_multiplier=1,
                      allow_small_or_imprecise_dtypes=True).then_inc(consts, 1)
            own.link(pool.memset(ident[:], 0.0))
            own.link(pool.affine_select(ident[:], ident[:], [[-1, P]], ALU.not_equal, 1.0, base=0, channel_multiplier=1))
            pool.memset(zeros_b[:], 0.0).then_inc(consts, 1)
            pool.memset(neg_ident[:], 0.0).then_inc(consts, 1)
            pool.wait_ge(pads_done, 16)
            own.link(pool.tensor_scalar(neg_ident[:], ident[:], -1.0, None, ALU.mult))
            pool.wait_ge(dve_setup, 2)
            own.link(pool.memset(zero, 0.0))
            pool.memset(agg[:, NP:NW], 0.0).then_inc(zero_done, 1)

            def clear(f, width):
                for i in turns(pool, STEPS, peel=0):
                    pool.wait_ge(z_ready, f * STEPS + i + 1)
                    pool.tensor_copy(agg[0:width, bass.ds(i * SC, SC)], zero[0:width].to_broadcast([width, SC]))\
                        .then_inc(zero_done, 1)

            def gather(q, k):
                table = table128 if PASS_WIDTH[q] == 128 else table64
                pool.indirect_dma_start(gathered[:, k, 0:PASS_WIDTH[q]], None, table,
                                        bass.IndirectOffsetOnAxis(ap=idx[:, k:k + 1], axis=0))\
                    .then_inc(gathered_s[k], 16)

            def gather_pass(q):
                for h in range(2):
                    pool.wait_ge(stored[h], 16 * (stored_at(STAGE_OF[q]) + STEPS // 2))
                for t in turns(pool, TURNS):
                    g = TURN0(q) + t
                    for k in range(K):
                        if k % 4 == 0:
                            pool.wait_ge(idx_ready, 4 * g + k // 4 + 1)
                        if not (q == 0 and isinstance(t, int)):
                            pool.wait_ge(summed, g * K + k - K + 1)
                            settle(pool)
                        gather(q, k)

            STAGE_OF = {q: f for f, q in PASS_AFTER.items()}
            for f in range(len(STAGES)):
                if f in ZERO_STAGES:
                    clear(f, 128 if f == 10 else 64)
                if f in PASS_AFTER and PASS_AFTER[f] < 7:
                    gather_pass(PASS_AFTER[f])
                if f == 10:
                    for h in range(2):
                        pool.wait_ge(stored[h], 16 * stored_at(12))
                    pool.wait_ge(summed, PASS0(7))
                    for t in turns(pool, TURNS):
                        for g in range(2):
                            c = 2 * t + g
                            if isinstance(t, int):
                                pool.wait_ge(idx_ready, 4 * TURN0(7) + 2 * g + 2)
                            else:
                                pool.wait_ge(idx_ready, 4 * TURN0(7) + c + 3)
                                settle(pool)
                            for k in range(GROUP):
                                gather(7, g * GROUP + k)

        @block.scalar
        def _(act):
            own = Own(act, act_own)
            eps = small[:, 0:1]

            def copy_idx(g, turn, h):
                act.copy(idx[:, 4 * h:4 * h + 4], src_i[:, bass.ds(turn * K + 4 * h, 4)]).then_inc(idx_ready, 1)

            act.wait_ge(rows_loaded, 16 * 5)
            act.wait_ge(dve_setup, 1)
            for h in range(4):
                copy_idx(0, 0, h)

            def prologue(f, m, i, h):
                name, source, wi, wo, finish = STAGES[f]
                cols = agg[0:wi, bass.ds(i * SC, SC)]
                if f > 0 or not isinstance(i, int):
                    act.wait_ge(z_used, m - 1)
                z = zbuf[0:wi, h, :]
                if source == "norm":
                    act.wait_ge(h_turned, NORM_STAGES.index(f) * STEPS + i + 1)
                    act.copy(z, turned[0:D]).then_inc(z_ready, 1)
                elif source == "norm_only":
                    act.wait_ge(h_turned, NORM_STAGES.index(f) * STEPS + i + 1)
                    act.copy(cols, turned[0:D]).then_inc(z_ready, 1)
                elif source == "affine":
                    if f < 3:
                        act.activation(h_in[:, bass.ds(i * SC, SC)], cols, ACT.Identity, bias=bn[:, 5:6],
                                       scale=bn[:, 4:5])
                    act.activation(z, cols, ACT.Identity, bias=bn[:, 5:6], scale=bn[:, 4:5]).then_inc(z_ready, 1)
                elif source == "relu":
                    act.activation(z, cols, ACT.Relu).then_inc(z_ready, 1)
                else:
                    act.copy(z, cols).then_inc(z_ready, 1)

            def start_agg(f, i):
                n = INIT_STAGES.index(f) * STEPS + i
                act.wait_ge(back_ready, n + 1)
                settle(act)
                wo = STAGES[f][3]
                act.copy(agg[0:wo, bass.ds(i * SC, SC)], back[0:wo]).then_inc(init_done, 1)

            def node_stage(f):
                init = f in INIT_STAGES
                for j in turns(act, STEPS // 2):
                    for h in range(2):
                        i = 2 * j + h
                        prologue(f, f * STEPS + i, i, h)
                        if init and not (isinstance(j, int) and h == 0):
                            start_agg(f, i - 1)
                if init:
                    start_agg(f, STEPS - 1)

            def layer_norm_root(s):
                act.wait_ge(ln_var, s + 1)
                act.activation(ln[:, 2, :], ln[:, 1, :], ACT.Sqrt, bias=eps, scale=1.0 / D).then_inc(ln_sd, 1)

            layer_norm_root(0)
            node_stage(0)

            act.wait_ge(stored[0], 16 * (STEPS // 2))
            act.wait_ge(stored[1], 16 * (STEPS // 2))
            act.wait_ge(moved, 32)
            act.wait_ge(pe_setup, 1)
            act.wait_ge(dve_setup, 3)
            for j in turns(act, TURNS // 2):
                for par in range(2):
                    t = 2 * j + par

                    def square(layer):
                        act.wait_ge(e_mm, 4 * t + 2 * layer + 1)
                        act.activation(e_sq, e_prod, ACT.Square, bias=centred[:, layer:layer + 1]).then_inc(e_act, 1)

                    def root(layer):
                        act.wait_ge(e_mm, 4 * t + 2 * layer + 2)
                        act.activation(e_sd, e_var, ACT.Sqrt, bias=eps).then_inc(e_act, 1)

                    def gelu(layer, out):
                        act.wait_ge(e_dve, 2 * t + layer + 1)
                        act.activation(out, e_y, ACT.Gelu, bias=mlp_b[:, layer, 2:3],
                                       scale=mlp_b[:, layer, 1:2]).then_inc(e_act, 1)

                    def next_idx(h):
                        act.wait_ge(summed, t * K + 4 * h + 4)
                        copy_idx(0, t + 1, h)

                    square(0)
                    next_idx(0)
                    root(0)
                    next_idx(1)
                    gelu(0, e_z)
                    next_idx(2)
                    square(1)
                    root(1)
                    next_idx(3)
                    if not isinstance(j, int):
                        act.wait_ge(e_stored[par], 16 * j)
                    gelu(1, e_out[:, par, :])

            def idx_pass(q):
                with act.Fori(0, TURNS) as t:
                    for h in range(4):
                        act.wait_ge(summed, PASS0(q) + t * K + 4 * h + 4)
                        copy_idx(q, t + 1, h)

            def agg_ready(q):
                act.wait_ge(added, PASS0(q + 1))

            for q in range(3):
                if q > 0:
                    idx_pass(q)
                    if q == 1:
                        act.wait_ge(deg_sum, 1)
                        act.activation(deg[:, 0:2, :], deg[:, 0:2, :], ACT.Sqrt).then_inc(deg_sd, 1)
                    if q == 2:
                        act.wait_ge(deg_sum, 2)
                        act.activation(deg[:, 2, :], deg[:, 2, :], ACT.Sqrt).then_inc(deg_sd, 1)
                agg_ready(q)
                for c in range(N_NODES // BN_PART):
                    if q or c:
                        act.wait_ge(prelu_done, q * (N_NODES // BN_PART) + c)
                    act.activation(prelu_pos, agg[0:D, c * BN_PART:(c + 1) * BN_PART], ACT.Relu,
                                   bias=l0_b[:, q:q + 1]).then_inc(relu_done, 1)
                act.wait_ge(bn_var, q + 1)
                act.activation(bn[:, 2:3], bn[:, 1:2], ACT.Sqrt, bias=eps[0:D]).then_inc(bn_sd, 1)
                act.wait_ge(bn_done, q + 1)
                if q == 0:
                    for h in range(2):
                        act.wait_ge(e_stored[h], 16 * (TURNS // 2))
                node_stage(q + 1)
            layer_norm_root(1)
            node_stage(4)
            for q, f in ((3, 5), (4, 6), (5, 7)):
                idx_pass(q)
                agg_ready(q)
                node_stage(f)
            layer_norm_root(2)
            node_stage(8)
            idx_pass(6)
            agg_ready(6)
            node_stage(9)
            layer_norm_root(3)
            node_stage(10)

            act.wait_ge(zero_done, len(ZERO_STAGES) * STEPS + 1)
            act.wait_ge(stored[0], 16 * stored_at(12))
            act.wait_ge(stored[1], 16 * stored_at(12))

            def rows_back(c):
                act.wait_ge(turned_back, c + 1)
                if not (isinstance(c, int) and c == 0):
                    act.wait_ge(summed, PASS0(7) + c * GROUP)
                act.copy(os_rows[:, :, :, 0:64], o_back.rearrange("p (j s w) -> p j s w", j=4, s=2))\
                    .then_inc(o_copied, 1)
                act.copy(os_rows[:, :, :, 64:128], s_back.rearrange("p (j s w) -> p j s w", j=4, s=2))
                act.wait_ge(m_turned, c + 1)
                act.copy(m_rows[:, :, :], m_back.rearrange("p (j s w) -> p j s w", j=4, s=2)[:, :, 1, :])\
                    .then_inc(rows_ready, 1)

            for t in turns(act, TURNS):
                first = isinstance(t, int)
                for h in range(2):
                    c = 2 * t + h
                    act.wait_ge(in3[h], 16 * IN3 * (t + 1))
                    if not (first and h == 0):
                        act.wait_ge(shift_ready, c)
                    act.activation(scaled[:, 0:GCOLS + 1], dst_pair[:, h, 0:GCOLS + 1], ACT.Copy, scale=BIG)\
                        .then_inc(scaled_ready, 1)
                    act.wait_ge(shift_ready, c + 1)
                    act.activation(rr, rr, ACT.Exp).then_inc(factor_ready, 1)
                    act.wait_ge(excess_ready, c + 1)
                    act.activation(pp, pp, ACT.Exp).then_inc(p_ready, 1)
                    if not (first and h == 0):
                        rows_back(c - 1)
                    act.wait_ge(values_ready, c + 1)
                    act.copy(idx[:, 8 * h:8 * h + 8], src_i[:, bass.ds((t + 1) * K + 8 * h, 8)]).then_inc(idx_ready, 1)
            rows_back(GROUPS - 1)
            act.wait_ge(fix_dve, 1)
            act.activation(fix[0:D, 2:4], fix[0:D, 2:4], ACT.Exp).then_inc(fix_act, 1)
            act.wait_ge(fix_dve, 3)
            node_stage(11)

        @block.vector
        def _(dve):
            own = Own(dve, dve_own)
            link = own.link

            dve.wait_ge(loaded, 16 * N_LOADS)
            dve.wait_ge(rows_loaded, 16 * 5)
            dve.wait_ge(consts, 4)
            link(dve.memset(small[:, 0:1], EPS))
            link(dve.memset(mlp[:], 0.0))
            for layer, rows in ((0, 6), (1, P)):
                mean = small[0:rows, 1 + layer:2 + layer]
                link(dve.tensor_reduce(mean, mlp_d[0:rows, layer, :], AX.X, ALU.add))
                link(dve.tensor_scalar(mean, mean, 1.0 / D, None, ALU.mult))
                link(dve.tensor_scalar(mlp_d[0:rows, layer, :], mlp_d[0:rows, layer, :], mean, None, ALU.subtract))
            for s in range(2):
                link(dve.tensor_copy(mlp[s * D:(s + 1) * D, 1, s * D:(s + 1) * D], mlp_d[s * D:(s + 1) * D, 1, :]))
            link(dve.memset(blk[:], 0.0))
            for s in range(2):
                link(dve.memset(blk[s * D:(s + 1) * D, s * D:(s + 1) * D], 1.0 / D))
            dve.sem_inc(dve_setup, 1)
            dve.tensor_tensor(dst_l[:], dst_i[:], agg[:, 0:CHUNKS].bitcast(I32), ALU.subtract).then_inc(dve_setup, 1)
            dve.wait_ge(dve_setup, 2)
            dve.wait_ge(pe_setup, 1)
            dve.tensor_tensor(centred[:], mlp_b[:, :, 0], setup_ps[:, 0:2], ALU.subtract).then_inc(dve_setup, 1)

            def layer_norm(s):
                sums, var, sd, rs = ln[:, 0, :], ln[:, 1, :], ln[:, 2, :], ln[:, 3, :]
                link(dve.tensor_reduce(sums, xn[:], AX.X, ALU.add))
                link(dve.tensor_scalar(sums, sums, 1.0 / D, None, ALU.mult))
                link(dve.tensor_tensor(hn, xn[:], sums.unsqueeze(2).to_broadcast([P, BLOCKS, D]), ALU.subtract))
                link(dve.tensor_tensor(sq, hn, hn, ALU.mult))
                dve.tensor_reduce(var, sq, AX.X, ALU.add).then_inc(ln_var, 1)
                dve.wait_ge(ln_sd, s + 1)
                link(dve.reciprocal(rs, sd))
                link(dve.tensor_tensor(hn, hn, rs.unsqueeze(2).to_broadcast([P, BLOCKS, D]), ALU.mult))

            def relu_steps(f, i, h):
                w = NORM_STAGES.index(f) * STEPS + i
                if f > 0 or not isinstance(i, int):
                    dve.wait_ge(h_turned, w - 1)
                dve.tensor_scalar(hblk[:, h], hn[:, bass.ds(i * SB, SB), :], 0.0, None, ALU.max).then_inc(h_ready, 1)
                if STAGES[f][4] == "scaled":
                    dve.wait_ge(h_ready, w + 1)

            def finish(f, i, h):
                name, source, wi, wo, how = STAGES[f]
                m = f * STEPS + i
                if how != "scaled":
                    dve.wait_ge(z_used, m + 1)
                ps = prod[h][:, 0:SB * wo].rearrange("p (b w) -> p b w", w=wo)
                rows = stage[:, h, 0:SB * wo].rearrange("p (b w) -> p b w", w=wo)
                part_b = lambda x: x[:, bass.ds(i * SB, SB)].unsqueeze(2).to_broadcast([P, SB, wo])
                x = xn[:, bass.ds(i * SB, SB), :]
                if not how.startswith("add") and not (f == 0 and isinstance(i, int)):
                    dve.wait_ge(stored[h], (stored_at(f) + half_step(i, h)) * 16)
                    if how == "attention" and not isinstance(i, int):
                        dve.wait_ge(w1_stored[h], half_step(i, h) * 16)
                if how == "table":
                    dve.tensor_copy(rows, ps).then_inc(finished, 1)
                elif how == "scaled":
                    dve.tensor_tensor(rows, hblk[:, h], part_b(deg[:, 1, :]), ALU.mult).then_inc(finished, 1)
                elif how == "attention":
                    link(dve.tensor_copy(rows, ps))
                    dve.tensor_copy(stage[:, h, SB * 128:SB * 192], prod_w1[h]).then_inc(finished, 1)
                elif how in ("gcn", "gcn_first"):
                    at_b = {4: 0, 5: 128, 6: 256}[f]
                    bias = l1_b[:, at_b:at_b + wo].unsqueeze(1).to_broadcast([P, SB, wo])
                    n = INIT_STAGES.index(f) * STEPS + i
                    if not (f == 4 and isinstance(i, int)):
                        dve.wait_ge(back_ready, n - 1)
                    if how == "gcn":
                        link(dve.tensor_tensor(rows, ps, part_b(deg[:, 0, :]), ALU.mult))
                        link(dve.tensor_tensor(rows, rows, bias, ALU.add))
                    else:
                        link(dve.tensor_tensor(rows, ps, bias, ALU.add))
                    dve.tensor_tensor(rows, rows, part_b(deg[:, 0, :]), ALU.mult).then_inc(finished, 1)
                elif how == "add":
                    dve.tensor_tensor(x, ps, x, ALU.add).then_inc(finished, 1)
                elif how in ("add_dinv", "add_norm_r"):
                    link(dve.tensor_tensor(rows, ps, part_b(deg[:, 0 if how == "add_dinv" else 2, :]), ALU.mult))
                    dve.tensor_tensor(x, x, rows, ALU.add).then_inc(finished, 1)
                else:
                    o, s = ps[:, :, 0:64], ps[:, :, 64:128]
                    r = rows[:, :, 0:64]
                    link(dve.tensor_scalar(r, s, 1e-30, None, ALU.max))
                    link(dve.reciprocal(r, r))
                    link(dve.tensor_tensor(r, o, r, ALU.mult))
                    dve.tensor_tensor(x, x, r, ALU.add).then_inc(finished, 1)

            def half_step(i, h):
                return i // 2 if isinstance(i, int) else half_of[0]

            half_of = [0]
            LINKS = {"table": 0, "scaled": 0, "attention": 1, "gcn": 2, "gcn_first": 1, "add": 0, "add_dinv": 1,
                     "add_norm_r": 1, "add_ratio": 3}

            def node_stage(f):
                name, source, wi, wo, how = STAGES[f]
                each = 2 * LINKS[how]
                for j in own.turns(STEPS // 2, each):
                    half_of[0] = j
                    for h in range(2):
                        i = 2 * j + h
                        if f in NORM_STAGES:
                            relu_steps(f, i, h)
                        finish(f, i, h)

            def build_onehot(q, n, col, k):
                if not (isinstance(n, int) and n < 4):
                    dve.wait_ge(summed, n - 3)
                scale = 1.0 if q == 6 else weight[:, bass.ds(col, 1)]
                dve.tensor_scalar(onehot[:, k % 4, :], iota[:], dst_l[:, bass.ds(col, 1)], scale, ALU.is_equal,
                                  ALU.mult).then_inc(onehot_ready, 1)

            def add_window(q, n, k, begin):
                dve.wait_ge(summed, n + 1)
                if not (isinstance(n, int) and n == 0):
                    dve.wait_ge(added, n)
                w = PASS_WIDTH[q]
                to = agg[0:w, bass.ds(begin, P)]
                dve.tensor_tensor(to, (window3[k % 2] if q == 7 else window[k % 4])[0:w], to, ALU.add).then_inc(added, 1)

            def window_begins(col, n):
                return nc.values_load_multi_w_load_instructions(
                    base[0:1, bass.ds(col, n)], engines=[mybir.EngineType.DVE], min_val=0, max_val=N_NODES,
                    skip_runtime_bounds_check_because="destinations are nodes")[1]

            def aggregate(q, t, beside=None):
                begin = window_begins(t * K, K)
                for k in range(K):
                    n = PASS0(q) + t * K + k
                    build_onehot(q, n, t * K + k, k)
                    if k >= 2:
                        add_window(q, n - 2, k - 2, begin[k - 2])
                    if beside and k in beside:
                        beside[k]()
                for k in (K - 2, K - 1):
                    add_window(q, PASS0(q) + t * K + k, k, begin[k])

            def bn_stage(q):
                dve.wait_ge(added, PASS0(q + 1))
                for c in range(N_NODES // BN_PART):
                    cols = agg[0:D, c * BN_PART:(c + 1) * BN_PART]
                    link(dve.tensor_scalar(prelu_neg, cols, l0_b[:, q:q + 1], 0.0, ALU.add, ALU.min))
                    dve.wait_ge(relu_done, q * (N_NODES // BN_PART) + c + 1)
                    link(dve.scalar_tensor_tensor(cols, prelu_neg, l0_prelu[:, q:q + 1], prelu_pos, ALU.mult, ALU.add))
                    if q > 0:
                        link(dve.tensor_tensor(cols, cols, h_in[:, c * BN_PART:(c + 1) * BN_PART], ALU.add))
                    for s in range(BN_PART // BN_CHUNK):
                        last = dve.bn_stats(stats[:, c * (BN_PART // BN_CHUNK) + s, :],
                                            cols[:, s * BN_CHUNK:(s + 1) * BN_CHUNK])
                        last.then_inc(prelu_done if s == BN_PART // BN_CHUNK - 1 else dve_stats, 1)
                dve.wait_ge(prelu_done, (q + 1) * (N_NODES // BN_PART))
                dve.wait_ge(dve_stats, (q + 1) * (N_NODES // BN_CHUNK - N_NODES // BN_PART))
                dve.bn_aggr(bn[:, 0:2], stats[:].rearrange("p a b -> p (a b)")).then_inc(bn_var, 1)
                dve.wait_ge(bn_sd, q + 1)
                link(dve.reciprocal(bn[:, 3:4], bn[:, 2:3]))
                link(dve.tensor_tensor(bn[:, 4:5], l0_gamma[:, q:q + 1], bn[:, 3:4], ALU.mult))
                link(dve.tensor_tensor(bn[:, 6:7], bn[:, 0:1], bn[:, 4:5], ALU.mult))
                dve.tensor_tensor(bn[:, 5:6], l0_beta[:, q:q + 1], bn[:, 6:7], ALU.subtract).then_inc(bn_done, 1)

            layer_norm(0)
            node_stage(0)

            dve.wait_ge(zero_done, STEPS + 1)
            for t in own.turns(TURNS, 2):
                def norm_edges(layer):
                    dve.wait_ge(e_act, 6 * t + 3 * layer + 2)
                    own.step(dve.reciprocal(e_sd, e_sd))
                    own.wait()
                    dve.scalar_tensor_tensor(e_y, e_prod, centred[:, layer:layer + 1], e_sd, ALU.add, ALU.mult)\
                        .then_inc(e_dve, 1)

                aggregate(0, t, {8: lambda: norm_edges(0)})
                norm_edges(1)
            bn_stage(0)
            node_stage(1)

            for q, ids in ((1, src_i), (2, dst_i)):
                dve.wait_ge(zero_done, (q + 1) * STEPS + 1)
                for h in range(2):
                    dve.wait_ge(stored[h], 16 * stored_at(q + 1))
                for t in own.turns(TURNS, 4):
                    cols = ids[:, bass.ds(t * K, K)]
                    if not (q == 1 and isinstance(t, int)):
                        dve.wait_ge(hist_used, (q - 1) * TURNS + t)
                    own.step(dve.tensor_scalar(hist_i[:, 0, :], cols, P - 1, None, ALU.bitwise_and))
                    own.step(dve.tensor_scalar(hist_i[:, 1, :], cols, 7, None, ALU.logical_shift_right))
                    own.wait()
                    own.step(dve.tensor_tensor(hist_lo, hist_i[:, 0, :].unsqueeze(2).to_broadcast([P, K, P]),
                                               iota[:].unsqueeze(1).to_broadcast([P, K, P]), ALU.is_equal))
                    own.step(dve.tensor_tensor(hist_hi, hist_i[:, 1, :].unsqueeze(2).to_broadcast([P, K, BLOCKS]),
                                               iota[:, 0:BLOCKS].unsqueeze(1).to_broadcast([P, K, BLOCKS]),
                                               ALU.is_equal))
                    own.wait()
                    dve.sem_inc(hist_ready, 1)
                    aggregate(q, t)
                dve.wait_ge(hist_closed, q)
                if q == 1:
                    link(dve.tensor_scalar(deg[:, 0, :], hist, 1.0, None, ALU.add))
                    dve.tensor_scalar(deg[:, 1, :], hist, 1.0, 1.0, ALU.max, ALU.add).then_inc(deg_sum, 1)
                    dve.wait_ge(deg_sd, 1)
                    link(dve.reciprocal(deg[:, 0:2, :], deg[:, 0:2, :]))
                else:
                    dve.tensor_scalar(deg[:, 2, :], hist, 1.0, 1.0, ALU.max, ALU.add).then_inc(deg_sum, 1)
                    dve.wait_ge(deg_sd, 2)
                    link(dve.reciprocal(deg[:, 2, :], deg[:, 2, :]))
                bn_stage(q)
                node_stage(q + 1)
            dve.wait_ge(finished, 4 * STEPS)
            layer_norm(1)
            node_stage(4)
            for q, f in ((3, 5), (4, 6), (5, 7)):
                dve.wait_ge(init_done, (q - 2) * STEPS)
                for t in turns(dve, TURNS):
                    aggregate(q, t)
                node_stage(f)
            dve.wait_ge(finished, 8 * STEPS)
            layer_norm(2)
            node_stage(8)
            dve.wait_ge(z_ready, 9 * STEPS)
            for t in turns(dve, TURNS):
                aggregate(6, t)
            node_stage(9)
            dve.wait_ge(finished, 10 * STEPS)
            layer_norm(3)
            node_stage(10)

            for h in range(2):
                dve.wait_ge(stored[h], 16 * stored_at(12))
                dve.wait_ge(w1_stored[h], 16 * (STEPS // 2))
            dve.wait_ge(zero_done, 4 * STEPS + 1)
            dve.wait_ge(next_loaded, 16)
            own.step(dve.tensor_tensor(weight[:], dst_i[:], next_i, ALU.not_equal))
            pd = dst_i[:].bitcast(F32)
            border = small[:, 5:6]
            own.step(dve.tensor_tensor(border, dst_i[:, 1:2], dst_l[:, 1:2], ALU.subtract))
            own.wait()
            own.step(dve.tensor_scalar(star_sel, dst_i[:].rearrange("p (c s) -> p c s", s=2)[:, :, 1], border, None,
                                       ALU.is_equal))
            own.wait()
            link(dve.tensor_tensor(star_sel, star_sel, weight[:].rearrange("p (c s) -> p c s", s=2)[:, :, 1], ALU.mult))
            link(dve.scalar_tensor_tensor(pd, dst_i[:], iota_p[:], dst_l[:], ALU.add, ALU.subtract))
            link(dve.memset(mm[:, 1, GCOLS:GCOLS + 1], 0.0))
            link(dve.memset(oo[:, 1, GCOLS - 1:GCOLS], 0.0))
            dve.memset(ss[:, 1, GCOLS - 1:GCOLS], 0.0).then_inc(star_ready, 1)
            dve.wait_ge(star_ready, 1)

            def spreads(t, h):
                dve.wait_ge(in3[h], 16 * IN3 * (t + 1))
                c = 2 * t + h
                for k in range(GROUP):
                    j, s = k // 2, k % 2
                    dve.tensor_scalar(spread[:, k, :], dst_ab[:, h, s, j * P:(j + 1) * P],
                                      pd[:, bass.ds(c * GROUP + k, 1)], None, ALU.is_equal).then_inc(spread_ready, 1)

            def running(c, h, first):
                m, m_old = mm[:, h, :], mm[:, 1 - h, :]
                if not first:
                    dve.wait_ge(m_turned, c - 1)
                own.step(dve.tensor_copy(m[:, 0:1], m_old[:, GCOLS:GCOLS + 1]))
                dve.wait_ge(scaled_ready, c + 1)
                own.step(dve.tensor_tensor(rr, scaled[:, 0:GCOLS], scaled[:, 1:GCOLS + 1], ALU.subtract))
                own.wait()
                dve.wait_ge(logits_ready, c + 1)
                link(dve.tensor_tensor_scan(m[:, 1:GCOLS + 1], rr, logit[h], m[:, 0:1], ALU.add, ALU.max))
                link(dve.tensor_tensor(rr, rr, m[:, 0:GCOLS], ALU.add))
                dve.tensor_tensor(rr, rr, m[:, 1:GCOLS + 1], ALU.subtract).then_inc(shift_ready, 1)
                dve.tensor_tensor(pp, logit[h], m[:, 1:GCOLS + 1], ALU.subtract).then_inc(excess_ready, 1)

            def sums(c, h):
                o, o_old, s, s_old = oo[:, h, :], oo[:, 1 - h, :], ss[:, h, :], ss[:, 1 - h, :]
                dve.wait_ge(factor_ready, c + 1)
                dve.wait_ge(p_ready, c + 1)
                own.step(dve.tensor_tensor_scan(s, rr, pp, s_old[:, GCOLS - 1:GCOLS], ALU.mult, ALU.add))
                dve.wait_ge(values_ready, c + 1)
                own.wait()
                dve.tensor_tensor(pw, pp, value, ALU.mult).then_inc(pw_ready, 1)
                dve.wait_ge(pw_ready, c + 1)
                dve.tensor_tensor_scan(o, rr, pw, o_old[:, GCOLS - 1:GCOLS], ALU.mult, ALU.add).then_inc(scans_done, 1)
                dve.wait_ge(scans_done, c + 1)

            def collect(c):
                begin = window_begins(c * GROUP, GROUP)
                for k in range(GROUP):
                    n = PASS0(7) + c * GROUP + k
                    build_onehot(7, n, c * GROUP + k, k)
                    if k >= 2:
                        add_window(7, n - 2, k - 2, begin[k - 2])
                for k in (GROUP - 2, GROUP - 1):
                    add_window(7, PASS0(7) + c * GROUP + k, k, begin[k])

            for t in own.turns(TURNS, 10):
                first = isinstance(t, int)
                spreads(t, 0)
                for h in range(2):
                    c = 2 * t + h
                    if not first:
                        collect(c - 2)
                    running(c, h, first)
                    if h == 0:
                        spreads(t, 1)
                    sums(c, h)
            collect(GROUPS - 2)
            collect(GROUPS - 1)
            dve.wait_ge(added, PASS0(8))

            dve.wait_ge(fix_pe, 1)
            m_a, f_a, f_b = fix[0:D, 0:1], fix[0:D, 2:3], fix[0:D, 3:4]
            cut, hold = fix[0:D, 4:5], fix[0:D, 5:6]
            link(dve.tensor_tensor(cut, end_a[0:D], border[0:D], ALU.is_equal))
            link(dve.tensor_scalar(hold, cut, 1.0, BIG, ALU.subtract, ALU.mult))
            link(dve.scalar_tensor_tensor(m_a, mm[0:D, 1, GCOLS:GCOLS + 1], cut, hold, ALU.mult, ALU.add))
            link(dve.tensor_copy(fix[0:D, 1:2], star))
            link(dve.tensor_tensor(fix[0:D, 6:7], m_a, fix[0:D, 1:2], ALU.max))
            link(dve.tensor_tensor(f_a, m_a, fix[0:D, 6:7], ALU.subtract))
            link(dve.tensor_tensor(f_b, fix[0:D, 1:2], fix[0:D, 6:7], ALU.subtract))
            dve.sem_inc(fix_dve, 1)
            link(dve.tensor_copy(spread[0:D, 0, 0:64], ident[0:D, 0:64]))
            link(dve.tensor_copy(spread[0:D, 0, 64:128], ident[0:D, 0:64]))
            link(dve.memset(spread[0:D, 1, 0:64], 0.0))
            link(dve.tensor_copy(spread[0:D, 1, 64:128], ident[0:D, 0:64]))
            dve.sem_inc(fix_dve, 1)
            dve.wait_ge(fix_pe, 2)
            link(dve.tensor_copy(fix[:, 8:11], fix_ps[:, 0:3]))
            link(dve.tensor_tensor(fix[:, 11:12], fix[:, 8:9], fix[:, 10:11], ALU.mult))
            at_border = window_begins(1, 1)[0]
            col = agg[:, bass.ds(at_border, 1)]
            link(dve.tensor_tensor(col, col, fix[:, 9:10], ALU.mult))
            dve.tensor_tensor(col, col, fix[:, 11:12], ALU.add).then_inc(fix_dve, 1)
            node_stage(11)
            dve.wait_ge(finished, 12 * STEPS)
            dve.sem_inc(out_ready, 1)

        @block.tensor
        def _(pe):
            WEIGHTS = {0: l0_w[:, 0, :], 1: l0_w[:, 1, :], 2: l0_w[:, 2, :], 4: l1_w1[:], 5: l1_w2[:], 6: l1_w3[:],
                       10: l3_w[:, 0:128]}

            pe.wait_ge(loaded, 16 * N_LOADS)
            pe.wait_ge(consts, 4)
            pe.wait_ge(dve_setup, 1)
            pe.matmul(setup_ps[:, 0:2], blk[:], mlp_b[:, :, 0], start=True, stop=True).then_inc(pe_setup, 1)
            pe.wait_ge(dve_setup, 3)
            pe.wait_ge(pads_done, 16)

            def turn_nodes(f, i, h):
                w = NORM_STAGES.index(f) * STEPS + i
                pe.wait_ge(h_ready, w + 1)
                if f > 0 or not (isinstance(i, int) and i == 0):
                    pe.wait_ge(z_ready, f * STEPS + i)
                settle(pe)
                for b in range(SB):
                    last = pe.transpose(turned[0:D, b * P:(b + 1) * P], hblk[:, h, b, :], ident[:])
                last.then_inc(h_turned, 1)
                if STAGES[f][1] == "norm_only":
                    pe.sem_inc(z_used, 1)

            def multiply(f, i, h):
                name, source, wi, wo, how = STAGES[f]
                m = f * STEPS + i
                w = WEIGHTS.get(f, ident[0:wi, 0:wo])
                pe.wait_ge(z_ready, m + 1)
                if f > 0 or not isinstance(i, int):
                    pe.wait_ge(finished, m - 1)
                for b in range(SB):
                    z = zbuf[0:wi, h, b * P:(b + 1) * P]
                    last = pe.matmul(prod[h][:, b * wo:(b + 1) * wo], z, w, start=True, stop=True)
                    if how == "attention":
                        last = pe.matmul(prod_w1[h][:, b * 64:(b + 1) * 64], z, l3_w[:, 128:192], start=True, stop=True)
                last.then_inc(z_used, 1)

            def turn_table(f, i, h):
                wo = STAGES[f][3]
                n = INIT_STAGES.index(f) * STEPS + i
                pe.wait_ge(finished, f * STEPS + i + 1)
                if not (isinstance(n, int) and n == 0):
                    pe.wait_ge(init_done, n)
                settle(pe)
                for b in range(SB):
                    last = pe.transpose(back[0:wo, b * P:(b + 1) * P], stage[:, h, b * wo:(b + 1) * wo], ident[:])
                last.then_inc(back_ready, 1)

            def node_stage(f):
                init = f in INIT_STAGES
                for j in turns(pe, STEPS // 2):
                    for h in range(2):
                        i = 2 * j + h
                        if f in NORM_STAGES:
                            turn_nodes(f, i, h)
                        if STAGES[f][1] != "norm_only":
                            multiply(f, i, h)
                        if init and not (isinstance(j, int) and h == 0):
                            turn_table(f, i - 1, 1 - h)
                if init:
                    turn_table(f, STEPS - 1, 1)

            def sum_pass(q, f, beside=None):
                pe.wait_ge(z_ready, (f + 1) * STEPS)
                w = PASS_WIDTH[q]
                for t in turns(pe, TURNS):
                    for k in range(K):
                        n = PASS0(q) + t * K + k
                        pe.wait_ge(onehot_ready, n + 1)
                        pe.wait_ge(gathered_s[k], 16 * (TURN0(q) + t + 1))
                        if not (isinstance(n, int) and n < 4):
                            pe.wait_ge(added, n - 3)
                        pe.matmul(window[k % 4][0:w], gathered[:, k, 0:w], onehot[:, k % 4, :], start=True,
                                  stop=True).then_inc(summed, 1)
                        if beside:
                            beside(t, k)

            def edge_step(t, par, j, k):
                if k not in (1, 5, 9, 13):
                    return
                if k == 1:
                    pe.wait_ge(e_loaded[par], 16 * (j + 1))
                    if not (isinstance(j, int) and par == 0):
                        pe.wait_ge(e_dve, 2 * t)
                    w, x, to = mlp[0:6, 0, :], e_in[:, par, :], e_prod
                elif k == 9:
                    pe.wait_ge(e_act, 6 * t + 3)
                    w, x, to = mlp[:, 1, :], e_z, e_prod
                else:
                    pe.wait_ge(e_act, 6 * t + (1 if k == 5 else 4))
                    w, x, to = blk[:], e_sq, e_var
                for c in range(2):
                    last = pe.matmul(to[:, c * 512:(c + 1) * 512], w, x[:, c * 512:(c + 1) * 512], start=True, stop=True)
                last.then_inc(e_mm, 1)

            def count_step(q):
                def step(t, k):
                    if k == 3:
                        pe.wait_ge(hist_ready, (q - 1) * TURNS + t + 1)
                        for x in range(K):
                            last = pe.matmul(hist, hist_lo[:, x, :], hist_hi[:, x, :], start=False, stop=False)
                        last.then_inc(hist_used, 1)
                return step

            node_stage(0)
            pe.wait_ge(z_ready, STEPS)
            pe.wait_ge(finished, STEPS)
            pe.wait_ge(moved, 32)
            for j in turns(pe, TURNS // 2):
                for par in range(2):
                    t = 2 * j + par
                    for k in range(K):
                        n = t * K + k
                        pe.wait_ge(onehot_ready, n + 1)
                        pe.wait_ge(gathered_s[k], 16 * (t + 1))
                        if not (isinstance(n, int) and n < 4):
                            pe.wait_ge(added, n - 3)
                        pe.matmul(window[k % 4][0:64], gathered[:, k, 0:64], onehot[:, k % 4, :], start=True,
                                  stop=True).then_inc(summed, 1)
                        edge_step(t, par, j, k)
            pe.wait_ge(e_act, 6 * TURNS)
            pe.wait_ge(e_dve, 2 * TURNS)
            node_stage(1)
            for q in (1, 2):
                if q == 2:
                    pe.wait_ge(deg_sum, 1)
                pe.wait_ge(finished, (q + 1) * STEPS)
                pe.matmul(hist, zeros_b[:], zeros_b[:, 0:BLOCKS], start=True, stop=False)
                sum_pass(q, q, count_step(q))
                pe.matmul(hist, zeros_b[:], zeros_b[:, 0:BLOCKS], start=False, stop=True).then_inc(hist_closed, 1)
                node_stage(q + 1)
            node_stage(4)
            for q, f in ((3, 5), (4, 6), (5, 7)):
                sum_pass(q, f - 1)
                node_stage(f)
            node_stage(8)
            sum_pass(6, 8)
            node_stage(9)
            node_stage(10)

            pe.wait_ge(finished, 11 * STEPS)
            pe.wait_ge(z_ready, 11 * STEPS)
            pe.wait_ge(star_ready, 1)
            pe.matmul(star, zeros_b[:, 0:64], zeros_b[:, 0:1], start=True, stop=False)

            def collect(c, k):
                j, s = k // 2, k % 2
                n = PASS0(7) + c * GROUP + k
                pe.wait_ge(rows_ready, c + 1)
                if s == 1:
                    pe.matmul(star, m_rows[:, j, :], star_sel[:, bass.ds(c * 4 + j, 1)], start=False, stop=False)
                pe.wait_ge(onehot_ready, n + 1)
                pe.wait_ge(added, n - 1)
                pe.matmul(window3[k % 2], os_rows[:, j, s, :], onehot[:, k % 4, :], start=True, stop=True)\
                    .then_inc(summed, 1)

            def logits(t, h, collected):
                c = 2 * t + h
                pe.wait_ge(in3[h], 16 * IN3 * (t + 1))
                if collected is not None:
                    pe.wait_ge(excess_ready, c - 1)
                pe.matmul(logit[h], ident[:], dt_in[:, h, :], start=True, stop=False, skip_group_check=True)
                for k in range(GROUP):
                    j, s = k // 2, k % 2
                    to = logit[h][s * D:(s + 1) * D, j * P:(j + 1) * P]
                    pe.wait_ge(gathered_s[h * GROUP + k], 16 * (TURN0(7) + t + 1))
                    pe.matmul(to, gathered[:, h * GROUP + k, 0:64], neg_ident[:], start=False, stop=False,
                              skip_group_check=True)
                    pe.wait_ge(spread_ready, c * GROUP + k + 1)
                    last = pe.matmul(to, w1_win[:, h * GROUP + k, :], spread[:, k, :], start=False, stop=k == GROUP - 1,
                                     skip_group_check=True)
                    if k == GROUP - 1:
                        last.then_inc(logits_ready, 1)
                    if collected is not None:
                        collect(collected, k)

            def turn_back(c, h):
                pe.wait_ge(scans_done, c + 1)
                if not (isinstance(c, int) and c == 0):
                    pe.wait_ge(rows_ready, c)
                for j in range(4):
                    pe.transpose(o_back[:, j * P:(j + 1) * P], oo[:, h, j * P:(j + 1) * P], ident[:])
                for j in range(4):
                    last = pe.transpose(s_back[:, j * P:(j + 1) * P], ss[:, h, j * P:(j + 1) * P], ident[:])
                last.then_inc(turned_back, 1)

            def turn_maxima(c, h):
                pe.wait_ge(o_copied, c + 1)
                for j in range(4):
                    last = pe.transpose(m_back[:, j * P:(j + 1) * P], mm[:, h, 1 + j * P:1 + (j + 1) * P], ident[:])
                last.then_inc(m_turned, 1)

            def values(t, h, first):
                c = 2 * t + h
                if not first:
                    pe.wait_ge(pw_ready, c)
                pe.matmul(value, ident[:], dt_in[:, h, :], start=True, stop=False, skip_group_check=True)
                for k in range(GROUP):
                    j, s = k // 2, k % 2
                    last = pe.matmul(value[s * D:(s + 1) * D, j * P:(j + 1) * P], gathered[:, h * GROUP + k, 64:128],
                                     ident[:], start=False, stop=k == GROUP - 1, skip_group_check=True)
                last.then_inc(values_ready, 1)

            for t in turns(pe, TURNS):
                first = isinstance(t, int)
                for h in range(2):
                    c = 2 * t + h
                    logits(t, h, None if first else c - 2)
                    if not (first and h == 0):
                        turn_back(c - 1, 1 - h)
                    values(t, h, first and h == 0)
                    if not (first and h == 0):
                        turn_maxima(c - 1, 1 - h)
            for k in range(GROUP):
                collect(GROUPS - 2, k)
            turn_back(GROUPS - 1, 1)
            turn_maxima(GROUPS - 1, 1)
            for k in range(GROUP):
                collect(GROUPS - 1, k)
            pe.matmul(star, zeros_b[:, 0:64], zeros_b[:, 0:1], start=False, stop=True).then_inc(fix_pe, 1)
            pe.wait_ge(fix_dve, 2)
            pe.wait_ge(fix_act, 1)
            pe.wait_ge(rows_ready, GROUPS)
            pe.matmul(fix_ps[:, 0:2], spread[0:D, 0, :], fix[0:D, 2:4], start=True, stop=True)
            pe.matmul(fix_ps[:, 2:3], ident[0:D, :], oo[0:D, 1, GCOLS - 1:GCOLS], start=True, stop=False)
            pe.matmul(fix_ps[:, 2:3], spread[0:D, 1, :], ss[0:D, 1, GCOLS - 1:GCOLS], start=False, stop=True)\
                .then_inc(fix_pe, 1)
            node_stage(11)


def _columns(v, fill):
    import numpy as np
    v = np.concatenate([v, np.full(EDGES - N_EDGES, fill, v.dtype)]).reshape(2, CHUNKS // 2, P)
    return np.ascontiguousarray(v.transpose(2, 1, 0).reshape(P, CHUNKS))


def kernel(**inputs):
    import numpy as np
    import concourse.bacc as bacc
    from concourse.bass_utils import run_bass_kernel_spmd

    i = {k: np.asarray(v) for k, v in inputs.items()}
    src = _columns(i["src"], N_NODES)
    dst = _columns(i["dst"], N_NODES)
    after = np.concatenate([i["dst"][1:], np.full(1, N_NODES, i["dst"].dtype)])
    row = np.concatenate([i["dst"], np.full(EDGES - N_EDGES, N_NODES, i["dst"].dtype)]).reshape(2, HALF)
    attr = np.concatenate([i["edge_attr_3"], np.zeros((EDGES - N_EDGES, 3), i["edge_attr_3"].dtype)])
    arrays = {
        "x": np.concatenate([i["x"], np.zeros((NP - N_NODES, D), i["x"].dtype)]),
        "src": np.concatenate([src, src[:, :K]], axis=1),
        "dst": dst,
        "dst_next": _columns(after, N_NODES),
        "ew": _columns(i["edge_weight"], 0.0),
        "base": dst[0:1, :],
        "dst_rows": np.concatenate([np.full((2, 1), -1, row.dtype), row], axis=1),
        "edge_attr": attr.reshape(2, HALF, 3).transpose(0, 2, 1).reshape(6, HALF),
        "l0_w": i["L0_gnn_W"], "l0_b": i["L0_gnn_b"].T, "l0_gamma": i["L0_gnn_bn_gamma"].T,
        "l0_beta": i["L0_gnn_bn_beta"].T, "l0_prelu": i["L0_gnn_prelu_a"],
        "l1_w1": i["L1_gnn_W1"].T, "l1_w2": i["L1_gnn_W2"].T, "l1_w3": i["L1_gnn_W3"].T,
        "l1_b": np.concatenate([i["L1_gnn_b1"], i["L1_gnn_b2"], i["L1_gnn_b3"]]),
        "l3_w1": i["L3_gnn_W1"], "l3_w2": i["L3_gnn_W2"], "l3_w3": i["L3_gnn_W3"],
        "wd1": i["L3_gnn_Wd1"], "wd2": i["L3_gnn_Wd2"],
        "mlp_b": np.stack([np.stack([i["L3_gnn_" + n + str(layer)] for n in ("bd", "g", "b")], axis=1)
                           for layer in (1, 2)], axis=1),
    }
    arrays = {"in_" + k: np.ascontiguousarray(v) for k, v in arrays.items()}
    nc = bacc.Bacc("TRN2", target_bir_lowering=False, num_devices=1)
    args = {k[3:]: nc.dram_tensor(k, v.shape, mybir.dt.from_np(v.dtype), kind="ExternalInput").ap()
            for k, v in arrays.items()}
    args["out"] = nc.dram_tensor("out", [N_NODES, D], F32, kind="ExternalOutput").ap()
    build(nc, args)
    r = run_bass_kernel_spmd(nc, [arrays], core_ids=[0])
    return r.results[0]["out"]
```

```python
from concourse import mybir
import concourse.bass as bass
from concourse.alu_op_type import AluOpType as ALU

N_NODES = 12500
N_EDGES = 212500
D = 64
P = 128
BLOCKS = -(-N_NODES // P)
NP = BLOCKS * P
NW = NP + P
K = 16
TURNS = -(-N_EDGES // (K * P))
CHUNKS = TURNS * K
EDGES = CHUNKS * P
HALF = EDGES // 2
GROUP = 8
GCOLS = GROUP // 2 * P
GROUPS = CHUNKS // GROUP
PASSES = 8
EDGE_PASSES = (3, 4, 5, 6)
UNIT = HALF // (len(EDGE_PASSES) * TURNS // 2)
SB = 7
STEPS = BLOCKS // SB
SC = SB * P
BN_CHUNK = 250
BN_PART = 1250
BN_PARTS = N_NODES // BN_PART
EPS = 1e-5
BIG = 1e30
assert BLOCKS == STEPS * SB and STEPS % 2 == 0 and N_NODES % BN_PART == 0 and N_EDGES < EDGES

assert UNIT <= 512 and UNIT * len(EDGE_PASSES) * (TURNS // 2) == HALF

F32 = mybir.dt.float32
BF16 = mybir.dt.bfloat16
I32 = mybir.dt.int32
ACT = mybir.ActivationFunctionType
AX = mybir.AxisListType

STAGES = [
    ("L0 layer 0 table", "norm", 64, 64, "table"),
    ("L0 layer 1 table", "affine", 64, 64, "table"),
    ("L0 layer 2 table", "affine", 64, 64, "table"),
    ("L0 residual", "affine", 64, 64, "add"),
    ("L1 layer 1 table", "norm", 64, 128, "gcn_first"),
    ("L1 layer 2 table", "relu", 128, 128, "gcn"),
    ("L1 layer 3 table", "relu", 128, 64, "gcn"),
    ("L1 residual", "relu", 64, 64, "add_dinv"),
    ("L2 table", "norm_only", 64, 64, "scaled"),
    ("L2 residual", "copy", 64, 64, "add_norm_r"),
    ("L3 tables", "norm", 64, 128, "attention"),
    ("L3 residual", "copy", 128, 128, "add_ratio"),
]
TABLE_STAGES = [n for n, s in enumerate(STAGES) if not s[4].startswith("add")]
NORM_STAGES = [n for n, s in enumerate(STAGES) if s[1].startswith("norm")]
INIT_STAGES = [n for n, s in enumerate(STAGES) if s[4].startswith("gcn")]
ZERO_STAGES = [0, 1, 2, 10]
PASS_AFTER = {0: 0, 1: 1, 2: 2, 4: 3, 5: 4, 6: 5, 8: 6, 10: 7}
PASS_WIDTH = [64, 64, 64, 128, 128, 64, 64, 128]


def turns(eng, n, peel=1, tail=0):
    for t in range(peel):
        yield t
    with eng.Fori(peel, n - tail) as t:
        yield t
    for t in range(n - tail, n):
        yield t


def at_start(t, n=1):
    return isinstance(t, int) and t < n


class Own:

    def __init__(self, eng, sem):
        self.eng, self.sem, self.base, self.off = eng, sem, 0, 0

    def step(self, ins):
        ins.then_inc(self.sem, 1)
        self.base += 1
        return self.base

    def wait(self, value=None):
        self.eng.wait_ge(self.sem, (self.base if value is None else value) + self.off)

    def link(self, ins):
        self.step(ins)
        self.wait()

    def turns(self, n, each, peel=1, tail=0):
        for t in range(peel):
            yield t
        start = self.base
        with self.eng.Fori(peel, n - tail) as t:
            self.off = (t - peel) * each
            yield t
            assert self.base == start + each, (self.base - start, each)
        self.off = 0
        self.base = start + each * (n - tail - peel)
        for t in range(n - tail, n):
            yield t


def build(nc, a):
    from contextlib import ExitStack

    ctx = ExitStack()
    with ctx:
        def sb(name, shape, dt=F32):
            return ctx.enter_context(nc.sbuf_tensor(name, shape, dt))

        def sem(name):
            return ctx.enter_context(nc.semaphore(name))

        def dram(name, shape, dt=F32):
            return nc.dram_tensor(name, shape, dt).ap()

        table64 = dram("table64", [NP, 64])
        table128 = dram("table128", [NP, 128])
        w1_table = dram("w1_table", [NW, 64])
        edge_d = dram("edge_d", [P, HALF])
        mask_d = dram("mask_d", [2, HALF])

        agg = sb("agg", [P, NW])
        wide = sb("wide", [P, NP])
        xn = sb("xn", [P, BLOCKS, D])
        src_i = sb("src_i", [P, CHUNKS + K], I32)
        dst_i = sb("dst_i", [P, CHUNKS], I32)
        dst_l = sb("dst_l", [P, CHUNKS])
        weight = sb("weight", [P, CHUNKS])
        base = sb("base", [1, CHUNKS], I32)
        ring = sb("ring", [P, 2560])
        stage = sb("stage", [P, 2, SB * 192])
        idx = sb("idx", [P, K], I32)
        ident = sb("ident", [P, P])
        zero_rows = sb("zero_rows", [P, 64])
        guard = sb("guard", [P, 1])
        iota = sb("iota", [P, P])
        iota_p = sb("iota_p", [P, 1])
        l0_w = sb("l0_w", [D, 3, D])
        l0_b = sb("l0_b", [D, 3])
        l0_gamma = sb("l0_gamma", [D, 3])
        l0_beta = sb("l0_beta", [D, 3])
        l0_prelu = sb("l0_prelu", [D, 3])
        l1_w1 = sb("l1_w1", [D, 128])
        l1_w2 = sb("l1_w2", [P, 128])
        l1_w3 = sb("l1_w3", [P, 64])
        l1_b = sb("l1_b", [P, 320])
        l3_w = sb("l3_w", [D, 192])
        mlp = sb("mlp", [P, 2, 128])
        mlp_d = sb("mlp_d", [P, 2, 64])
        mlp_b = sb("mlp_b", [P, 2, 3])
        centred = sb("centred", [P, 2])
        small = sb("small", [P, 16])
        stats = sb("stats", [D, N_NODES // BN_CHUNK, 6])
        bn = sb("bn", [D, 8])
        l0_minus = sb("l0_minus", [D, 2, 3])
        ln = sb("ln", [P, 4, BLOCKS])
        deg = sb("deg", [P, 3, BLOCKS])
        zeros_b = sb("zeros_b", [P, P], BF16)
        blk = sb("blk", [P, P])
        hist_i = sb("hist_i", [P, 2, K], I32)
        end_a = sb("end_a", [P, 1], I32)

        gathered = ring[:, 0:K * P].rearrange("p (k w) -> p k w", k=K)
        onehot = ring[:, K * P:2560].rearrange("p (k w) -> p k w", k=4)
        zbuf = ring[:, 0:2 * SC].rearrange("p (h c) -> p h c", h=2)
        ln_stats = ring[:, 2 * SC:2 * SC + 6 * BLOCKS].rearrange("p (b w) -> p b w", w=6)
        relu_neg = [ring[0:D, x * BN_PART:(x + 1) * BN_PART] for x in range(2)]
        relu_pos = [stage[0:D, x, 0:BN_PART] for x in range(2)]
        hist_lo = stage[:, 0, 0:1024].bitcast(BF16).rearrange("p (k w) -> p k w", k=K)
        hist_hi = stage[:, 1, 0:K * BLOCKS // 2].bitcast(BF16).rearrange("p (k w) -> p k w", k=K)

        hblk = wide[:, 6 * UNIT:6 * UNIT + 2 * SB * D].rearrange("p (h b d) -> p h b d", h=2, d=D)
        h_in = wide[0:D, :]
        e_in = wide[0:6, 0:UNIT]
        e_sq, e_sd, e_y, e_z, e_out = [wide[:, n * UNIT:(n + 1) * UNIT] for n in range(1, 6)]
        at = [0]

        def part(n):
            at[0] += n
            return wide[:, at[0] - n:at[0]]

        dt_in = part(2 * GCOLS).rearrange("p (h c) -> p h c", h=2)
        dst_ab = part(4 * GCOLS).bitcast(I32).rearrange("p (h s c) -> p h s c", h=2, s=2)
        mask = part(2 * GCOLS).rearrange("p (h c) -> p h c", h=2)
        w1_win = part(K * 64).rearrange("p (k w) -> p k w", k=K)
        spread = part(GROUP * P).rearrange("p (k w) -> p k w", k=GROUP)
        rr = part(GCOLS)
        pp = part(GCOLS)
        pw = part(GCOLS)
        mm = part(2 * (GCOLS + 2)).rearrange("p (h c) -> p h c", h=2)
        oo = part(2 * GCOLS).rearrange("p (h c) -> p h c", h=2)
        ss = part(2 * GCOLS).rearrange("p (h c) -> p h c", h=2)
        ends = [onehot, part(4 * P).rearrange("p (k w) -> p k w", k=4)]
        sflat = stage[:].rearrange("p h c -> p (h c)")
        os_rows = [x.rearrange("p (j s w) -> p j s w", j=4, s=2) for x in (sflat[:, 0:GROUP * P], part(GROUP * P))]
        m_rows = [sflat[:, 1024 + 256 * x:1280 + 256 * x].rearrange("p (j w) -> p j w", j=4) for x in range(2)]
        assert at[0] <= NP, at[0]
        next_i = sflat[:, 0:CHUNKS].bitcast(I32)
        star_sel = sflat[:, CHUNKS:CHUNKS + CHUNKS // 2]
        mask_in = [agg[:, n * CHUNKS:(n + 1) * CHUNKS].bitcast(I32) for n in (1, 2)]
        mask_out = agg[:, 3 * CHUNKS:4 * CHUNKS]
        fix = sflat[:, 2560:2576]


        psum = ctx.enter_context(nc.psum_tensor("psum", [P, 8, 512], F32))
        flat = psum.rearrange("p b c -> p (b c)")
        prod = [flat[:, 1024 * h:1024 * h + SC] for h in range(2)]
        prod_w1 = [psum[:, 4 + h, 0:SB * 64] for h in range(2)]
        back = flat[:, 2048:2048 + SC]
        turned = flat[:, 3072:3072 + SC]
        window = [psum[:, 4 + k, 0:P] for k in range(4)]
        window3 = [psum[:, 5 + k, 0:P] for k in range(2)]
        hist = psum[:, 0, 0:BLOCKS]
        e_prod, e_var = psum[:, 0, 0:UNIT], psum[:, 1, 0:UNIT]
        logit = [psum[:, 0, :], psum[:, 1, :]]
        value = psum[:, 2, :]
        o_back, s_back, m_back = psum[:, 3, :], psum[:, 4, :], psum[:, 3, :]
        star = psum[0:D, 7, 0:1]
        setup_ps = psum[:, 0, 0:8]
        fix_ps = psum[:, 3, 0:4]

        x_loaded = sem("x_loaded")
        loaded = sem("loaded")
        rows_loaded = sem("rows_loaded")
        mask_loaded = sem("mask_loaded")
        mask_made = sem("mask_made")
        mask_stored = sem("mask_stored")
        pads_done = sem("pads_done")
        moved = sem("moved")
        consts = sem("consts")
        pool_own = sem("pool_own")
        dve_own = sem("dve_own")
        act_own = sem("act_own")
        dve_setup = sem("dve_setup")
        pe_setup = sem("pe_setup")
        ln_var = sem("ln_var")
        ln_sd = sem("ln_sd")
        h_ready = sem("h_ready")
        h_turned = sem("h_turned")
        z_ready = sem("z_ready")
        z_used = sem("z_used")
        finished = sem("finished")
        stored = [sem("stored0"), sem("stored1")]
        w1_stored = [sem("w1_stored0"), sem("w1_stored1")]
        back_ready = sem("back_ready")
        init_done = sem("init_done")
        zero_done = sem("zero_done")
        idx_ready = sem("idx_ready")
        gathered_s = [sem(f"gathered{k}") for k in range(K)]
        onehot_ready = sem("onehot_ready")
        summed = sem("summed")
        added = sem("added")
        relu_done = sem("relu_done")
        prelu_done = sem("prelu_done")
        bn_var = sem("bn_var")
        bn_sd = sem("bn_sd")
        bn_done = sem("bn_done")
        e_loaded = sem("e_loaded")
        e_mm = sem("e_mm")
        e_act = sem("e_act")
        e_dve = sem("e_dve")
        e_stored = sem("e_stored")
        hist_ready = sem("hist_ready")
        hist_used = sem("hist_used")
        hist_closed = sem("hist_closed")
        deg_sum = sem("deg_sum")
        deg_sd = sem("deg_sd")
        in3 = [sem("in3_0"), sem("in3_1")]
        star_ready = sem("star_ready")
        spread_ready = sem("spread_ready")
        ends_ready = sem("ends_ready")
        logits_ready = sem("logits_ready")
        values_ready = sem("values_ready")
        shift_ready = sem("shift_ready")
        excess_ready = sem("excess_ready")
        factor_ready = sem("factor_ready")
        p_ready = sem("p_ready")
        scans_done = sem("scans_done")
        turned_back = sem("turned_back")
        o_copied = sem("o_copied")
        m_turned = sem("m_turned")
        rows_ready = sem("rows_ready")
        pw_ready = sem("pw_ready")
        next_loaded = sem("next_loaded")
        fix_dve = sem("fix_dve")
        fix_pe = sem("fix_pe")
        fix_act = sem("fix_act")
        out_stored = sem("out_stored")

        N_LOADS = 21
        IN3 = GROUP + 4
        PASS0 = lambda q: q * CHUNKS
        TURN0 = lambda q: q * TURNS
        EDGE_TURN0 = lambda q: (q - EDGE_PASSES[0]) * TURNS

        passed = {}

        def settle(eng):
            if eng not in passed:
                passed[eng] = sem(f"passed{len(passed)}")
            eng.sem_inc(passed[eng], 1)

        def stored_at(f):
            return sum(1 for n in TABLE_STAGES if n < f) * (STEPS // 2)

        block = ctx.enter_context(nc.Block())

        @block.sync
        def _(sp):
            sp.dma_start(xn[:], a["x"].rearrange("(b p) d -> p b d", p=P)).then_inc(x_loaded, 16)
            small_loads = [
                (l0_w[:], a["l0_w"].rearrange("l i o -> i l o")),
                (l0_b[:], a["l0_b"]), (l0_gamma[:], a["l0_gamma"]), (l0_beta[:], a["l0_beta"]),
                (l0_prelu[:], a["l0_prelu"].partition_broadcast(D)),
                (l1_w1[:], a["l1_w1"]), (l1_w2[:], a["l1_w2"]), (l1_w3[:], a["l1_w3"]),
                (l1_b[:], a["l1_b"].partition_broadcast(P)),
                (l3_w[:, 0:64], a["l3_w2"]), (l3_w[:, 64:128], a["l3_w3"]), (l3_w[:, 128:192], a["l3_w1"]),
                (mlp_d[0:3, 0, :], a["wd1"]), (mlp_d[3:6, 0, :], a["wd1"]),
                (mlp_d[0:D, 1, :], a["wd2"]), (mlp_d[D:P, 1, :], a["wd2"]),
                (mlp_b[0:D, 0, :], a["mlp_b"][:, 0, :]), (mlp_b[D:P, 0, :], a["mlp_b"][:, 0, :]),
                (mlp_b[0:D, 1, :], a["mlp_b"][:, 1, :]), (mlp_b[D:P, 1, :], a["mlp_b"][:, 1, :]),
                (end_a[:], a["dst_rows"][0:1, HALF:HALF + 1].partition_broadcast(P).rearrange("p a c -> p (a c)")),
            ]
            for to, of in small_loads:
                sp.dma_start(to, of).then_inc(loaded, 16)
            sp.dma_start(src_i[:], a["src"]).then_inc(rows_loaded, 16)
            sp.dma_start(dst_i[:], a["dst"]).then_inc(rows_loaded, 16)
            sp.dma_start(weight[:], a["ew"]).then_inc(rows_loaded, 16)
            sp.dma_start(base[:], a["base"]).then_inc(rows_loaded, 16)
            sp.dma_start(agg[:, 0:CHUNKS].bitcast(I32), a["base"].partition_broadcast(P).rearrange("p a c -> p (a c)"))\
                .then_inc(rows_loaded, 16)
            for n in range(2):
                for s in range(2):
                    sp.dma_start(mask_in[n][s * D:(s + 1) * D, :], a["dst_rows"][s:s + 1, n:n + HALF]
                                 .rearrange("o (r c) -> (o r) c", c=CHUNKS)).then_inc(mask_loaded, 16)
            assert len(small_loads) == N_LOADS
            sp.wait_ge(dve_setup, 1)
            sp.dma_start(mlp[0:3, 0, 0:64], mlp_d[0:3, 0, :]).then_inc(moved, 16)
            sp.dma_start(mlp[3:6, 0, 64:128], mlp_d[3:6, 0, :]).then_inc(moved, 16)
            sp.wait_ge(consts, 4)
            sp.dma_start(w1_table[NP:NW, :], zero_rows[:]).then_inc(pads_done, 16)
            sp.wait_ge(mask_made, 2)
            sp.dma_start(mask_d.rearrange("s (r c) -> (s r) c", c=CHUNKS), mask_out).then_inc(mask_stored, 16)

            def store_tables(f):
                name, source, wi, wo, finish = STAGES[f]
                table = (table128 if wo == 128 else table64).rearrange("(i b p) w -> i p b w", b=SB, p=P)
                w1 = w1_table[0:NP, :].rearrange("(i b p) w -> i p b w", b=SB, p=P)
                with sp.Fori(0, STEPS // 2) as j:
                    for h in range(2):
                        i = 2 * j + h
                        sp.wait_ge(finished, f * STEPS + i + 1)
                        rows = stage[:, h, :]
                        sp.dma_start(table[bass.ds(i, 1)].rearrange("o p b w -> (o p) b w"),
                                     rows[:, 0:SB * wo].rearrange("p (b w) -> p b w", b=SB)).then_inc(stored[h], 16)
                        if finish == "attention":
                            sp.dma_start(w1[bass.ds(i, 1)].rearrange("o p b w -> (o p) b w"),
                                         rows[:, SB * 128:SB * 192].rearrange("p (b w) -> p b w", b=SB))\
                                .then_inc(w1_stored[h], 16)

            store_tables(0)

            def edge_load(u):
                sp.dma_start(e_in, a["edge_attr"][:, bass.ds(u * UNIT, UNIT)]).then_inc(e_loaded, 16)

            def edge_store(u):
                sp.wait_ge(e_act, 6 * u + 6)
                sp.dma_start(edge_d[:, bass.ds(u * UNIT, UNIT)], e_out).then_inc(e_stored, 16)

            def edge_pass(f):
                sp.wait_ge(z_ready, (f + 1) * STEPS)
                start, n = EDGE_TURN0(PASS_AFTER[f]) // 2, TURNS // 2
                edge_load(start)
                with sp.Fori(start, start + n - 1) as u:
                    sp.wait_ge(e_mm, 4 * u + 1)
                    edge_load(u + 1)
                    edge_store(u)
                edge_store(start + n - 1)

            for f in TABLE_STAGES[1:]:
                store_tables(f)
                if PASS_AFTER[f] in EDGE_PASSES:
                    edge_pass(f)
            sp.wait_ge(e_stored, 16 * EDGE_TURN0(7) // 2)

            for h in range(2):
                sp.wait_ge(stored[h], 16 * stored_at(12))
                sp.wait_ge(w1_stored[h], 16 * (STEPS // 2))
            sp.dma_start(next_i, a["dst_next"]).then_inc(next_loaded, 16)
            sp.wait_ge(pads_done, 16)
            sp.wait_ge(mask_stored, 16)
            sp.wait_ge(zero_done, len(ZERO_STAGES) * STEPS + 1)

            def attention_loads(c, h):
                begin = nc.values_load_multi_w_load_instructions(
                    base[0:1, bass.ds(c * GROUP, GROUP)], engines=[mybir.EngineType.SP], min_val=0, max_val=N_NODES,
                    skip_runtime_bounds_check_because="destinations are nodes")[1]
                if not (isinstance(c, int) and c < 2):
                    sp.wait_ge(values_ready, c - 1)
                for k in range(GROUP):
                    sp.dma_start(w1_win[:, h * GROUP + k, :], w1_table[bass.ds(begin[k], P), :]).then_inc(in3[h], 16)
                sp.dma_start(dt_in[:, h, :], edge_d[:, bass.ds(c * GCOLS, GCOLS)]).then_inc(in3[h], 16)
                if not (isinstance(c, int) and c < 2):
                    sp.wait_ge(spread_ready, 2 * (c - 1))
                    sp.wait_ge(shift_ready, c - 1)
                sp.dma_start(dst_ab[:, h], a["dst_rows"][:, bass.ds(c * GCOLS + 1, GCOLS)].partition_broadcast(P))\
                    .then_inc(in3[h], 16)
                for s in range(2):
                    sp.dma_start(mask[s * D:(s + 1) * D, h, :],
                                 mask_d[s:s + 1, bass.ds(c * GCOLS, GCOLS)].partition_broadcast(D)
                                 .rearrange("p a c -> p (a c)")).then_inc(in3[h], 16)

            for t in turns(sp, TURNS):
                for h in range(2):
                    c = 2 * t + h
                    attention_loads(c, h)

            rows = a["out"][0:(STEPS - 1) * SC, :].rearrange("(i b p) d -> i p b d", b=SB, p=P)
            with sp.Fori(0, STEPS - 1) as i:
                sp.wait_ge(finished, (len(STAGES) - 1) * STEPS + i + 1)
                sp.dma_start(rows[bass.ds(i, 1)].rearrange("o p b d -> (o p) b d"),
                             xn[:, bass.ds(i * SB, SB), :]).then_inc(out_stored, 16)
            sp.wait_ge(finished, len(STAGES) * STEPS)
            full = N_NODES // P
            sp.dma_start(a["out"][(STEPS - 1) * SC:full * P, :].rearrange("(b p) d -> p b d", p=P),
                         xn[:, (STEPS - 1) * SB:full, :]).then_inc(out_stored, 16)
            sp.dma_start(a["out"][full * P:N_NODES, :], xn[0:N_NODES - full * P, full, :]).then_inc(out_stored, 16)
            sp.wait_ge(out_stored, 16 * (STEPS + 1))

        @block.gpsimd
        def _(pool):
            own = Own(pool, pool_own)
            pool.iota(iota[:], [[1, P]], base=0, channel_multiplier=0,
                      allow_small_or_imprecise_dtypes=True).then_inc(consts, 1)
            pool.iota(iota_p[:], [[0, 1]], base=0, channel_multiplier=1,
                      allow_small_or_imprecise_dtypes=True).then_inc(consts, 1)
            own.link(pool.memset(ident[:], 0.0))
            own.link(pool.affine_select(ident[:], ident[:], [[-1, P]], ALU.not_equal, 1.0, base=0, channel_multiplier=1))
            pool.memset(zeros_b[:], 0.0).then_inc(consts, 1)
            pool.memset(zero_rows[:], 0.0).then_inc(consts, 1)
            pool.wait_ge(dve_setup, 2)
            pool.memset(agg[:, NP:NW], 0.0).then_inc(zero_done, 1)
            pool.wait_ge(mask_stored, 16)

            def clear(f, width):
                for i in range(STEPS):
                    pool.wait_ge(z_ready, f * STEPS + i + 1)
                    pool.memset(agg[0:width, i * SC:(i + 1) * SC], 0.0).then_inc(zero_done, 1)

            def gather(q, k):
                table = table128 if PASS_WIDTH[q] == 128 else table64
                pool.indirect_dma_start(gathered[:, k, 0:PASS_WIDTH[q]], None, table,
                                        bass.IndirectOffsetOnAxis(ap=idx[:, k:k + 1], axis=0))\
                    .then_inc(gathered_s[k], 16)

            def gather_pass(q):
                for h in range(2):
                    pool.wait_ge(stored[h], 16 * (stored_at(STAGE_OF[q]) + STEPS // 2))
                for t in turns(pool, TURNS):
                    g = TURN0(q) + t
                    for k in range(K):
                        if k % 4 == 0:
                            pool.wait_ge(idx_ready, 4 * g + k // 4 + 1)
                        if not (q == 0 and isinstance(t, int)):
                            pool.wait_ge(summed, g * K + k - K + 1)
                            settle(pool)
                        gather(q, k)

            STAGE_OF = {q: f for f, q in PASS_AFTER.items()}
            for f in range(len(STAGES)):
                if f in ZERO_STAGES:
                    clear(f, 128 if f == 10 else 64)
                if f in PASS_AFTER and PASS_AFTER[f] < 7:
                    gather_pass(PASS_AFTER[f])
                if f == 10:
                    for h in range(2):
                        pool.wait_ge(stored[h], 16 * stored_at(12))
                    pool.wait_ge(summed, PASS0(7))
                    for t in turns(pool, TURNS):
                        for g in range(2):
                            c = 2 * t + g
                            if isinstance(t, int):
                                pool.wait_ge(idx_ready, 4 * TURN0(7) + 2 * g + 2)
                            else:
                                pool.wait_ge(idx_ready, 4 * TURN0(7) + c + 3)
                                settle(pool)
                            for k in range(GROUP):
                                gather(7, g * GROUP + k)

        @block.scalar
        def _(act):
            own = Own(act, act_own)
            eps = small[:, 0:1]

            def copy_idx(g, turn, h):
                act.copy(idx[:, 4 * h:4 * h + 4], src_i[:, bass.ds(turn * K + 4 * h, 4)]).then_inc(idx_ready, 1)

            def prologue(f, m, i, h):
                name, source, wi, wo, finish = STAGES[f]
                cols = agg[0:wi, bass.ds(i * SC, SC)]
                if f > 0 or not at_start(i, 2):
                    act.wait_ge(z_used, m - 1)
                z = zbuf[0:wi, h, :]
                if source == "norm":
                    act.wait_ge(h_turned, NORM_STAGES.index(f) * STEPS + i + 1)
                    act.copy(z, turned[0:D]).then_inc(z_ready, 1)
                elif source == "norm_only":
                    act.wait_ge(h_turned, NORM_STAGES.index(f) * STEPS + i + 1)
                    act.copy(cols, turned[0:D]).then_inc(z_ready, 1)
                elif source == "affine":
                    if f < 3:
                        act.activation(h_in[:, bass.ds(i * SC, SC)], cols, ACT.Identity, bias=bn[:, 5:6],
                                       scale=bn[:, 4:5])
                    act.activation(z, cols, ACT.Identity, bias=bn[:, 5:6], scale=bn[:, 4:5]).then_inc(z_ready, 1)
                elif source == "relu":
                    act.activation(z, cols, ACT.Relu).then_inc(z_ready, 1)
                elif f == len(STAGES) - 1:
                    act.activation(z, cols, ACT.Identity, bias=guard[:]).then_inc(z_ready, 1)
                else:
                    act.copy(z, cols).then_inc(z_ready, 1)

            def start_agg(f, i):
                n = INIT_STAGES.index(f) * STEPS + i
                act.wait_ge(back_ready, n + 1)
                settle(act)
                wo = STAGES[f][3]
                act.copy(agg[0:wo, bass.ds(i * SC, SC)], back[0:wo]).then_inc(init_done, 1)

            def node_stage(f):
                init = f in INIT_STAGES
                prologue(f, f * STEPS, 0, 0)
                for j in turns(act, STEPS // 2, tail=1):
                    for h in range(2):
                        i = 2 * j + h
                        if not (isinstance(i, int) and i == STEPS - 1):
                            prologue(f, f * STEPS + i + 1, i + 1, 1 - h)
                        if init and not at_start(i):
                            start_agg(f, i - 1)
                if init:
                    start_agg(f, STEPS - 1)

            def layer_norm_root(s):
                act.wait_ge(ln_var, s + 1)
                act.activation(ln[:, 2, :], ln[:, 1, :], ACT.Sqrt, bias=eps, scale=1.0 / D).then_inc(ln_sd, 1)

            layer_norm_root(0)
            act.wait_ge(rows_loaded, 16 * 5)
            act.wait_ge(dve_setup, 1)
            for h in range(4):
                copy_idx(0, 0, h)
            node_stage(0)

            def edge_step(par, g, n):
                if n == 0:
                    act.wait_ge(e_mm, 2 * g + 1)
                    act.activation(e_sq, e_prod, ACT.Square, bias=centred[:, par:par + 1]).then_inc(e_act, 1)
                elif n == 1:
                    act.wait_ge(e_mm, 2 * g + 2)
                    act.activation(e_sd, e_var, ACT.Sqrt, bias=eps).then_inc(e_act, 1)
                else:
                    act.wait_ge(e_dve, g + 1)
                    if par and not (isinstance(g, int) and g == 1):
                        act.wait_ge(e_stored, 8 * (g - 1))
                    act.activation((e_z, e_out)[par], e_y, ACT.Gelu, bias=mlp_b[:, par, 2:3],
                                   scale=mlp_b[:, par, 1:2]).then_inc(e_act, 1)

            def edge_idx_pass(q):
                for j in turns(act, TURNS // 2, peel=q == EDGE_PASSES[0]):
                    for par in range(2):
                        t = 2 * j + par
                        for h in range(4):
                            if h != 2:
                                edge_step(par, EDGE_TURN0(q) + t, min(h, 2))
                            act.wait_ge(summed, PASS0(q) + t * K + 4 * h + 4)
                            copy_idx(q, t + 1, h)

            def idx_pass(q):
                with act.Fori(0, TURNS) as t:
                    for h in range(4):
                        act.wait_ge(summed, PASS0(q) + t * K + 4 * h + 4)
                        copy_idx(q, t + 1, h)

            def agg_ready(q):
                act.wait_ge(added, PASS0(q + 1))

            for q in range(3):
                idx_pass(q)
                if q > 0:
                    if q == 1:
                        act.wait_ge(deg_sum, 1)
                        act.activation(deg[:, 0:2, :], deg[:, 0:2, :], ACT.Sqrt).then_inc(deg_sd, 1)
                    if q == 2:
                        act.wait_ge(deg_sum, 2)
                        act.activation(deg[:, 2, :], deg[:, 2, :], ACT.Sqrt).then_inc(deg_sd, 1)
                agg_ready(q)
                for c in range(BN_PARTS):
                    if q or c > 1:
                        act.wait_ge(prelu_done, q * BN_PARTS + c - 1)
                    cols = agg[0:D, c * BN_PART:(c + 1) * BN_PART]
                    act.activation(relu_pos[c % 2], cols, ACT.Relu, bias=l0_b[:, q:q + 1])
                    act.activation(relu_neg[c % 2], cols, ACT.Relu, bias=l0_minus[:, 0, q:q + 1], scale=-1.0)\
                        .then_inc(relu_done, 1)
                act.wait_ge(bn_var, q + 1)
                act.activation(bn[:, 2:3], bn[:, 1:2], ACT.Sqrt, bias=eps[0:D]).then_inc(bn_sd, 1)
                act.wait_ge(bn_done, q + 1)
                node_stage(q + 1)
            layer_norm_root(1)
            node_stage(4)
            act.wait_ge(pe_setup, 1)
            act.wait_ge(dve_setup, 3)
            for q, f in ((3, 5), (4, 6), (5, 7)):
                edge_idx_pass(q)
                agg_ready(q)
                node_stage(f)
            layer_norm_root(2)
            node_stage(8)
            edge_idx_pass(6)
            agg_ready(6)
            node_stage(9)
            layer_norm_root(3)
            node_stage(10)

            act.wait_ge(zero_done, len(ZERO_STAGES) * STEPS + 1)
            act.wait_ge(stored[0], 16 * stored_at(12))
            act.wait_ge(stored[1], 16 * stored_at(12))

            def sums_back(c, x):
                act.wait_ge(turned_back, c + 1)
                if not (isinstance(c, int) and c < 2):
                    act.wait_ge(summed, PASS0(7) + (c - 1) * GROUP)
                act.copy(os_rows[x][:, :, :, 0:64], o_back.rearrange("p (j s w) -> p j s w", j=4, s=2))\
                    .then_inc(o_copied, 1)
                act.copy(os_rows[x][:, :, :, 64:128], s_back.rearrange("p (j s w) -> p j s w", j=4, s=2))

            def maxima_back(c, x):
                act.wait_ge(m_turned, c + 1)
                act.copy(m_rows[x], m_back.rearrange("p (j s w) -> p j s w", j=4, s=2)[:, :, 1, :])\
                    .then_inc(rows_ready, 1)

            for t in turns(act, TURNS):
                for h in range(2):
                    c = 2 * t + h
                    act.wait_ge(values_ready, c + 1)
                    act.copy(idx[:, 8 * h:8 * h + 8], src_i[:, bass.ds((t + 1) * K + 8 * h, 8)]).then_inc(idx_ready, 1)
                    if not at_start(c):
                        sums_back(c - 1, 1 - h)
                    act.wait_ge(shift_ready, c + 1)
                    act.activation(rr, rr, ACT.Exp).then_inc(factor_ready, 1)
                    act.wait_ge(excess_ready, c + 1)
                    act.activation(pp, pp, ACT.Exp).then_inc(p_ready, 1)
                    if not at_start(c):
                        maxima_back(c - 1, 1 - h)
            sums_back(GROUPS - 1, 1)
            maxima_back(GROUPS - 1, 1)
            act.wait_ge(fix_dve, 1)
            act.activation(fix[0:D, 2:4], fix[0:D, 2:4], ACT.Exp).then_inc(fix_act, 1)
            act.wait_ge(fix_dve, 3)
            node_stage(11)

        @block.vector
        def _(dve):
            own = Own(dve, dve_own)
            link = own.link

            def set_up():
                dve.wait_ge(loaded, 16 * N_LOADS)
                dve.wait_ge(rows_loaded, 16 * 5)
                dve.wait_ge(consts, 4)
                link(dve.memset(guard[0:D], 0.0))
                link(dve.memset(guard[D:P], 1e-30))
                link(dve.memset(mlp[:], 0.0))
                for layer, rows in ((0, 6), (1, P)):
                    mean = small[0:rows, 1 + layer:2 + layer]
                    link(dve.tensor_reduce(mean, mlp_d[0:rows, layer, :], AX.X, ALU.add))
                    link(dve.tensor_scalar(mean, mean, 1.0 / D, None, ALU.mult))
                    link(dve.tensor_scalar(mlp_d[0:rows, layer, :], mlp_d[0:rows, layer, :], mean, None, ALU.subtract))
                for s in range(2):
                    link(dve.tensor_copy(mlp[s * D:(s + 1) * D, 1, s * D:(s + 1) * D], mlp_d[s * D:(s + 1) * D, 1, :]))
                link(dve.memset(blk[:], 0.0))
                for s in range(2):
                    link(dve.memset(blk[s * D:(s + 1) * D, s * D:(s + 1) * D], 1.0 / D))
                dve.sem_inc(dve_setup, 1)
                link(dve.tensor_scalar(l3_w[:, 0:64], l3_w[:, 0:64], -1.0, None, ALU.mult))
                link(dve.tensor_scalar(l0_minus[:, 0, :], l0_b[:], -1.0, None, ALU.mult))
                link(dve.tensor_scalar(l0_minus[:, 1, :], l0_prelu[:], -1.0, None, ALU.mult))
                dve.tensor_tensor(dst_l[:], dst_i[:], agg[:, 0:CHUNKS].bitcast(I32), ALU.subtract).then_inc(dve_setup, 1)
                dve.wait_ge(dve_setup, 2)
                dve.wait_ge(mask_loaded, 64)
                dve.tensor_tensor(mask_out, mask_in[0], mask_in[1], ALU.subtract).then_inc(mask_made, 1)
                dve.wait_ge(mask_made, 1)
                dve.tensor_scalar(mask_out, mask_out, BIG, None, ALU.mult).then_inc(mask_made, 1)
                dve.wait_ge(pe_setup, 1)
                dve.tensor_tensor(centred[:], mlp_b[:, :, 0], setup_ps[:, 0:2], ALU.subtract).then_inc(dve_setup, 1)

            def norm_stats(i):
                of, to = xn[:, bass.ds(i * SB, SB), :], ln_stats[:, bass.ds(i * SB, SB), :]
                for b in range(SB):
                    last = dve.bn_stats(to[:, b, :], of[:, b, :])
                own.step(last)

            def layer_norm():
                mean, var, sd, rs = [ln[:, n, :] for n in range(4)]
                m_0, s_0, m_1, s_1 = [ln_stats[:, :, n] for n in (1, 2, 4, 5)]
                own.wait()
                own.step(dve.tensor_tensor(mean, m_0, m_1, ALU.add))
                own.step(dve.tensor_tensor(rs, m_0, m_1, ALU.subtract))
                own.step(dve.tensor_tensor(var, s_0, s_1, ALU.add))
                own.wait()
                own.step(dve.tensor_scalar(mean, mean, 0.5, None, ALU.mult))
                link(dve.tensor_tensor(rs, rs, rs, ALU.mult))
                dve.scalar_tensor_tensor(var, rs, D / 4, var, ALU.mult, ALU.add).then_inc(ln_var, 1)
                norms[0] += 1
                dve.wait_ge(ln_sd, norms[0])
                link(dve.reciprocal(rs, sd))

            norms = [0]

            def relu_steps(f, i, h):
                w = NORM_STAGES.index(f) * STEPS + i
                if f > 0 or not at_start(i, 2):
                    dve.wait_ge(h_turned, w - 1)
                if STAGES[f][4] == "scaled" and not at_start(i):
                    dve.wait_ge(finished, f * STEPS + i - 1)
                per_node = lambda x: x[:, bass.ds(i * SB, SB)].unsqueeze(2).to_broadcast([P, SB, D])
                link(dve.tensor_tensor(hblk[:, h], xn[:, bass.ds(i * SB, SB), :], per_node(ln[:, 0, :]), ALU.subtract))
                dve.scalar_tensor_tensor(hblk[:, h], hblk[:, h], 0.0, per_node(ln[:, 3, :]), ALU.max, ALU.mult)\
                    .then_inc(h_ready, 1)

            def finish(f, i, h):
                name, source, wi, wo, how = STAGES[f]
                m = f * STEPS + i
                if how == "scaled":
                    dve.wait_ge(h_ready, NORM_STAGES.index(f) * STEPS + i + 1)
                else:
                    dve.wait_ge(z_used, m + 1)
                ps = prod[h][:, 0:SB * wo].rearrange("p (b w) -> p b w", w=wo)
                rows = stage[:, h, 0:SB * wo].rearrange("p (b w) -> p b w", w=wo)
                part_b = lambda x: x[:, bass.ds(i * SB, SB)].unsqueeze(2).to_broadcast([P, SB, wo])
                x = xn[:, bass.ds(i * SB, SB), :]
                if not how.startswith("add") and not (f == 0 and at_start(i, 2)):
                    dve.wait_ge(stored[h], (stored_at(f) + half_step(i, h)) * 16)
                    if how == "attention" and not at_start(i, 2):
                        dve.wait_ge(w1_stored[h], half_step(i, h) * 16)
                if how == "table":
                    dve.tensor_copy(rows, ps).then_inc(finished, 1)
                elif how == "scaled":
                    dve.tensor_tensor(rows, hblk[:, h], part_b(deg[:, 1, :]), ALU.mult).then_inc(finished, 1)
                elif how == "attention":
                    link(dve.tensor_copy(rows, ps))
                    dve.tensor_copy(stage[:, h, SB * 128:SB * 192], prod_w1[h]).then_inc(finished, 1)
                elif how in ("gcn", "gcn_first"):
                    at_b = {4: 0, 5: 128, 6: 256}[f]
                    bias = l1_b[:, at_b:at_b + wo].unsqueeze(1).to_broadcast([P, SB, wo])
                    n = INIT_STAGES.index(f) * STEPS + i
                    if not (f == 4 and at_start(i, 2)):
                        dve.wait_ge(back_ready, n - 1)
                    if how == "gcn":
                        link(dve.tensor_tensor(rows, ps, part_b(deg[:, 0, :]), ALU.mult))
                        link(dve.tensor_tensor(rows, rows, bias, ALU.add))
                    else:
                        link(dve.tensor_tensor(rows, ps, bias, ALU.add))
                    dve.tensor_tensor(rows, rows, part_b(deg[:, 0, :]), ALU.mult).then_inc(finished, 1)
                elif how == "add":
                    dve.tensor_tensor(x, ps, x, ALU.add).then_inc(finished, 1)
                elif how in ("add_dinv", "add_norm_r"):
                    link(dve.tensor_tensor(rows, ps, part_b(deg[:, 0 if how == "add_dinv" else 2, :]), ALU.mult))
                    dve.tensor_tensor(x, x, rows, ALU.add).then_inc(finished, 1)
                else:
                    o, s = ps[:, :, 0:64], ps[:, :, 64:128]
                    r = rows[:, :, 0:64]
                    link(dve.reciprocal(r, s))
                    link(dve.tensor_tensor(r, o, r, ALU.mult))
                    dve.tensor_tensor(x, x, r, ALU.add).then_inc(finished, 1)

            def half_step(i, h):
                return i // 2 if isinstance(i, int) else half_of[0]

            half_of = [0]
            LINKS = {"table": 0, "scaled": 0, "attention": 1, "gcn": 2, "gcn_first": 1, "add": 0, "add_dinv": 1,
                     "add_norm_r": 1, "add_ratio": 2}

            def node_stage(f):
                name, source, wi, wo, how = STAGES[f]
                stats_too = f + 1 in NORM_STAGES
                each = 2 * (LINKS[how] + (f in NORM_STAGES) + stats_too)
                ahead = 1 if how == "scaled" else 2
                if f in NORM_STAGES:
                    for i in range(ahead):
                        relu_steps(f, i, i)
                for j in own.turns(STEPS // 2, each, tail=1):
                    half_of[0] = j
                    for h in range(2):
                        i = 2 * j + h
                        if f in NORM_STAGES and not (isinstance(i, int) and i + ahead >= STEPS):
                            relu_steps(f, i + ahead, (h + ahead) % 2)
                        finish(f, i, h)
                        if stats_too:
                            dve.wait_ge(finished, f * STEPS + i + 1)
                            norm_stats(i)

            def build_onehot(q, n, col, k):
                if not (isinstance(n, int) and n < 4):
                    dve.wait_ge(summed, n - 3)
                scale = 1.0 if q == 6 else weight[:, bass.ds(col, 1)]
                dve.tensor_scalar(onehot[:, k % 4, :], iota[:], dst_l[:, bass.ds(col, 1)], scale, ALU.is_equal,
                                  ALU.mult).then_inc(onehot_ready, 1)

            def add_window(q, n, k, begin):
                dve.wait_ge(summed, n + 1)
                if not (isinstance(n, int) and n == 0):
                    dve.wait_ge(added, n)
                w = PASS_WIDTH[q]
                to = agg[0:w, bass.ds(begin, P)]
                dve.tensor_tensor(to, (window3[k % 2] if q == 7 else window[k % 4])[0:w], to, ALU.add).then_inc(added, 1)

            def window_begins(col, n):
                return nc.values_load_multi_w_load_instructions(
                    base[0:1, bass.ds(col, n)], engines=[mybir.EngineType.DVE], min_val=0, max_val=N_NODES,
                    skip_runtime_bounds_check_because="destinations are nodes")[1]

            def aggregate(q, t, beside=None):
                begin = window_begins(t * K, K)
                for k in range(K):
                    n = PASS0(q) + t * K + k
                    build_onehot(q, n, t * K + k, k)
                    if k >= 2:
                        add_window(q, n - 2, k - 2, begin[k - 2])
                    if beside and k in beside:
                        beside[k]()
                for k in (K - 2, K - 1):
                    add_window(q, PASS0(q) + t * K + k, k, begin[k])

            def bn_stage(q):
                dve.wait_ge(added, PASS0(q + 1))
                for c in range(BN_PARTS):
                    cols = agg[0:D, c * BN_PART:(c + 1) * BN_PART]
                    dve.wait_ge(relu_done, q * BN_PARTS + c + 1)
                    dve.scalar_tensor_tensor(cols, relu_neg[c % 2], l0_minus[:, 1, q:q + 1], relu_pos[c % 2], ALU.mult,
                                             ALU.add).then_inc(prelu_done, 1)
                    dve.wait_ge(prelu_done, q * BN_PARTS + c + 1)
                    if q > 0:
                        link(dve.tensor_tensor(cols, cols, h_in[:, c * BN_PART:(c + 1) * BN_PART], ALU.add))
                    for s in range(BN_PART // BN_CHUNK):
                        last = dve.bn_stats(stats[:, c * (BN_PART // BN_CHUNK) + s, :],
                                            cols[:, s * BN_CHUNK:(s + 1) * BN_CHUNK])
                own.step(last)
                own.wait()
                dve.bn_aggr(bn[:, 0:2], stats[:].rearrange("p a b -> p (a b)")).then_inc(bn_var, 1)
                dve.wait_ge(bn_sd, q + 1)
                link(dve.reciprocal(bn[:, 3:4], bn[:, 2:3]))
                link(dve.tensor_tensor(bn[:, 4:5], l0_gamma[:, q:q + 1], bn[:, 3:4], ALU.mult))
                link(dve.tensor_tensor(bn[:, 6:7], bn[:, 0:1], bn[:, 4:5], ALU.mult))
                dve.tensor_tensor(bn[:, 5:6], l0_beta[:, q:q + 1], bn[:, 6:7], ALU.subtract).then_inc(bn_done, 1)

            def edge_pass(q):
                for j in own.turns(TURNS // 2, 2, peel=q == EDGE_PASSES[0]):
                    for par in range(2):
                        t = 2 * j + par

                        def norm_edges():
                            g = EDGE_TURN0(q) + t
                            dve.wait_ge(e_act, 3 * g + 2)
                            own.step(dve.reciprocal(e_sd, e_sd))
                            own.wait()
                            dve.scalar_tensor_tensor(e_y, e_prod, centred[:, par:par + 1], e_sd, ALU.add, ALU.mult)\
                                .then_inc(e_dve, 1)

                        aggregate(q, t, {8: norm_edges})

            def edge_buffers_free(q):
                dve.wait_ge(e_act, 3 * EDGE_TURN0(q))
                dve.wait_ge(e_stored, 16 * EDGE_TURN0(q) // 2)

            link(dve.memset(small[:, 0:1], EPS))
            dve.wait_ge(x_loaded, 16)
            for i in own.turns(STEPS, 1):
                norm_stats(i)
            layer_norm()
            set_up()
            node_stage(0)

            dve.wait_ge(zero_done, STEPS + 1)
            for t in turns(dve, TURNS):
                aggregate(0, t)
            bn_stage(0)
            node_stage(1)

            for q, ids in ((1, src_i), (2, dst_i)):
                dve.wait_ge(zero_done, (q + 1) * STEPS + 1)
                for h in range(2):
                    dve.wait_ge(stored[h], 16 * stored_at(q + 1))
                for t in own.turns(TURNS, 4):
                    cols = ids[:, bass.ds(t * K, K)]
                    if not (q == 1 and isinstance(t, int)):
                        dve.wait_ge(hist_used, (q - 1) * TURNS + t)
                    own.step(dve.tensor_scalar(hist_i[:, 0, :], cols, P - 1, None, ALU.bitwise_and))
                    own.step(dve.tensor_scalar(hist_i[:, 1, :], cols, 7, None, ALU.logical_shift_right))
                    own.wait()
                    own.step(dve.tensor_tensor(hist_lo, hist_i[:, 0, :].unsqueeze(2).to_broadcast([P, K, P]),
                                               iota[:].unsqueeze(1).to_broadcast([P, K, P]), ALU.is_equal))
                    own.step(dve.tensor_tensor(hist_hi, hist_i[:, 1, :].unsqueeze(2).to_broadcast([P, K, BLOCKS]),
                                               iota[:, 0:BLOCKS].unsqueeze(1).to_broadcast([P, K, BLOCKS]),
                                               ALU.is_equal))
                    own.wait()
                    dve.sem_inc(hist_ready, 1)
                    aggregate(q, t)
                dve.wait_ge(hist_closed, q)
                if q == 1:
                    link(dve.tensor_scalar(deg[:, 0, :], hist, 1.0, None, ALU.add))
                    dve.tensor_scalar(deg[:, 1, :], hist, 1.0, 1.0, ALU.max, ALU.add).then_inc(deg_sum, 1)
                    dve.wait_ge(deg_sd, 1)
                    link(dve.reciprocal(deg[:, 0:2, :], deg[:, 0:2, :]))
                else:
                    dve.tensor_scalar(deg[:, 2, :], hist, 1.0, 1.0, ALU.max, ALU.add).then_inc(deg_sum, 1)
                    dve.wait_ge(deg_sd, 2)
                    link(dve.reciprocal(deg[:, 2, :], deg[:, 2, :]))
                bn_stage(q)
                node_stage(q + 1)
            layer_norm()
            node_stage(4)
            for q, f in ((3, 5), (4, 6), (5, 7)):
                dve.wait_ge(init_done, (q - 2) * STEPS)
                edge_pass(q)
                node_stage(f)
            layer_norm()
            node_stage(8)
            dve.wait_ge(z_ready, 9 * STEPS)
            edge_pass(6)
            node_stage(9)
            layer_norm()
            node_stage(10)
            edge_buffers_free(7)

            for h in range(2):
                dve.wait_ge(stored[h], 16 * stored_at(12))
                dve.wait_ge(w1_stored[h], 16 * (STEPS // 2))
            dve.wait_ge(zero_done, 4 * STEPS + 1)
            dve.wait_ge(next_loaded, 16)
            own.step(dve.tensor_tensor(weight[:], dst_i[:], next_i, ALU.not_equal))
            pd = dst_i[:].bitcast(F32)
            border = small[:, 5:6]
            own.step(dve.tensor_tensor(border, dst_i[:, 1:2], dst_l[:, 1:2], ALU.subtract))
            own.wait()
            own.step(dve.tensor_scalar(star_sel, dst_i[:].rearrange("p (c s) -> p c s", s=2)[:, :, 1], border, None,
                                       ALU.is_equal))
            own.wait()
            link(dve.tensor_tensor(star_sel, star_sel, weight[:].rearrange("p (c s) -> p c s", s=2)[:, :, 1], ALU.mult))
            link(dve.scalar_tensor_tensor(pd, dst_i[:], iota_p[:], dst_l[:], ALU.add, ALU.subtract))
            link(dve.scalar_tensor_tensor(weight[:], dst_l[:], 1.0, weight[:], ALU.add, ALU.mult))
            link(dve.tensor_scalar(weight[:], weight[:], -1.0, None, ALU.add))
            link(dve.memset(mm[:, 0, 0:1], 0.0))
            link(dve.memset(oo[:, 1, GCOLS - 1:GCOLS], 0.0))
            dve.memset(ss[:, 1, GCOLS - 1:GCOLS], 0.0).then_inc(star_ready, 1)
            dve.wait_ge(star_ready, 1)

            def spread_out(c, h, t, s):
                if s == 0:
                    dve.wait_ge(in3[h], 16 * IN3 * (t + 1))
                    if not at_start(c):
                        dve.wait_ge(logits_ready, c)
                nodes = pd[:, bass.ds(c * GROUP, GROUP)].rearrange("p (j s) -> p s j", s=2)[:, s]
                dve.tensor_tensor(spread[:, 4 * s:4 * s + 4, :], dst_ab[:, h, s, :].rearrange("p (j w) -> p j w", j=4),
                                  nodes.unsqueeze(2).to_broadcast([P, 4, P]), ALU.is_equal).then_inc(spread_ready, 1)

            def build_ends(c, half):
                if not (isinstance(c, int) and c == 0):
                    dve.wait_ge(summed, PASS0(7) + (c - 1) * GROUP + 4 * half + 4)
                col = weight[:, bass.ds(c * GROUP + 4 * half, 4)]
                dve.tensor_tensor(ends[half], iota[:].unsqueeze(1).to_broadcast([P, 4, P]),
                                  col.unsqueeze(2).to_broadcast([P, 4, P]), ALU.is_equal).then_inc(ends_ready, 1)

            def attention_group(t, h):
                c = 2 * t + h
                if isinstance(t, int) and t == 0:
                    def add(k):
                        pass
                else:
                    begin = window_begins((c - 2) * GROUP, GROUP)

                    def add(k):
                        add_window(7, PASS0(7) + (c - 2) * GROUP + k, k, begin[k])

                m = mm[:, h, :]
                o, o_old, s, s_old = oo[:, h, :], oo[:, 1 - h, :], ss[:, h, :], ss[:, 1 - h, :]
                if not (isinstance(c, int) and c < 2):
                    dve.wait_ge(m_turned, c - 1)
                dve.wait_ge(in3[h], 16 * IN3 * (t + 1))
                dve.wait_ge(logits_ready, c + 1)
                own.step(dve.tensor_tensor_scan(m[:, 1:GCOLS + 1], mask[:, h, :], logit[h], m[:, 0:1], ALU.add,
                                                ALU.max))
                add(0)
                own.wait()
                own.step(dve.tensor_tensor(rr, mask[:, h, :], m[:, 0:GCOLS], ALU.add))
                add(1)
                own.wait()
                dve.tensor_tensor(rr, rr, m[:, 1:GCOLS + 1], ALU.subtract).then_inc(shift_ready, 1)
                dve.tensor_tensor(pp, logit[h], m[:, 1:GCOLS + 1], ALU.subtract).then_inc(excess_ready, 1)
                own.step(dve.tensor_copy(mm[:, 1 - h, 0:1], m[:, GCOLS:GCOLS + 1]))
                add(2)
                last = isinstance(c, int) and c == GROUPS - 1
                if not last:
                    spread_out(c + 1, 1 - h, t + h, 0)
                add(3)
                if not last:
                    spread_out(c + 1, 1 - h, t + h, 1)
                if not at_start(c):
                    build_ends(c - 1, 0)
                add(4)
                dve.wait_ge(factor_ready, c + 1)
                dve.wait_ge(p_ready, c + 1)
                own.step(dve.tensor_tensor_scan(s, rr, pp, s_old[:, GCOLS - 1:GCOLS], ALU.mult, ALU.add))
                add(5)
                dve.wait_ge(values_ready, c + 1)
                dve.tensor_tensor(pw, pp, value, ALU.mult).then_inc(pw_ready, 1)
                add(6)
                own.wait()
                dve.wait_ge(pw_ready, c + 1)
                if not at_start(c):
                    dve.wait_ge(scans_done, c)
                dve.tensor_tensor_scan(o, rr, pw, o_old[:, GCOLS - 1:GCOLS], ALU.mult, ALU.add).then_inc(scans_done, 1)
                add(7)
                if not at_start(c):
                    build_ends(c - 1, 1)

            spread_out(0, 0, 0, 0)
            spread_out(0, 0, 0, 1)
            for t in own.turns(TURNS, 8, tail=1):
                for h in range(2):
                    attention_group(t, h)
            begin = window_begins((GROUPS - 2) * GROUP, 2 * GROUP)
            for k in range(2 * GROUP):
                if k in (4, 8):
                    build_ends(GROUPS - 1, k // 4 - 1)
                add_window(7, PASS0(8) - 2 * GROUP + k, k, begin[k])
            dve.wait_ge(added, PASS0(8))
            dve.wait_ge(scans_done, GROUPS)

            dve.wait_ge(fix_pe, 1)
            m_a, f_a, f_b = fix[0:D, 0:1], fix[0:D, 2:3], fix[0:D, 3:4]
            cut, hold = fix[0:D, 4:5], fix[0:D, 5:6]
            link(dve.tensor_tensor(cut, end_a[0:D], border[0:D], ALU.is_equal))
            link(dve.tensor_scalar(hold, cut, 1.0, BIG, ALU.subtract, ALU.mult))
            link(dve.scalar_tensor_tensor(m_a, mm[0:D, 1, GCOLS:GCOLS + 1], cut, hold, ALU.mult, ALU.add))
            link(dve.tensor_copy(fix[0:D, 1:2], star))
            link(dve.tensor_tensor(fix[0:D, 6:7], m_a, fix[0:D, 1:2], ALU.max))
            link(dve.tensor_tensor(f_a, m_a, fix[0:D, 6:7], ALU.subtract))
            link(dve.tensor_tensor(f_b, fix[0:D, 1:2], fix[0:D, 6:7], ALU.subtract))
            dve.sem_inc(fix_dve, 1)
            link(dve.tensor_copy(spread[0:D, 0, 0:64], ident[0:D, 0:64]))
            link(dve.tensor_copy(spread[0:D, 0, 64:128], ident[0:D, 0:64]))
            link(dve.memset(spread[0:D, 1, 0:64], 0.0))
            link(dve.tensor_copy(spread[0:D, 1, 64:128], ident[0:D, 0:64]))
            dve.sem_inc(fix_dve, 1)
            dve.wait_ge(fix_pe, 2)
            link(dve.tensor_copy(fix[:, 8:11], fix_ps[:, 0:3]))
            link(dve.tensor_tensor(fix[:, 11:12], fix[:, 8:9], fix[:, 10:11], ALU.mult))
            at_border = window_begins(1, 1)[0]
            col = agg[:, bass.ds(at_border, 1)]
            link(dve.tensor_tensor(col, col, fix[:, 9:10], ALU.mult))
            dve.tensor_tensor(col, col, fix[:, 11:12], ALU.add).then_inc(fix_dve, 1)
            node_stage(11)

        @block.tensor
        def _(pe):
            WEIGHTS = {0: l0_w[:, 0, :], 1: l0_w[:, 1, :], 2: l0_w[:, 2, :], 4: l1_w1[:], 5: l1_w2[:], 6: l1_w3[:],
                       10: l3_w[:, 0:128]}

            pe.wait_ge(loaded, 16 * N_LOADS)
            pe.wait_ge(consts, 4)
            pe.wait_ge(dve_setup, 1)
            pe.matmul(setup_ps[:, 0:2], blk[:], mlp_b[:, :, 0], start=True, stop=True).then_inc(pe_setup, 1)
            pe.wait_ge(dve_setup, 3)
            pe.wait_ge(pads_done, 16)

            def turn_nodes(f, i, h):
                w = NORM_STAGES.index(f) * STEPS + i
                pe.wait_ge(h_ready, w + 1)
                if f > 0 or not (isinstance(i, int) and i == 0):
                    pe.wait_ge(z_ready, f * STEPS + i)
                settle(pe)
                for b in range(SB):
                    last = pe.transpose(turned[0:D, b * P:(b + 1) * P], hblk[:, h, b, :], ident[:])
                last.then_inc(h_turned, 1)
                if STAGES[f][1] == "norm_only":
                    pe.sem_inc(z_used, 1)

            def multiply(f, i, h):
                name, source, wi, wo, how = STAGES[f]
                m = f * STEPS + i
                w = WEIGHTS.get(f)
                pe.wait_ge(z_ready, m + 1)
                if f > 0 or not at_start(i, 2):
                    pe.wait_ge(finished, m - 1)
                if how.startswith("add"):
                    settle(pe)
                for b in range(SB):
                    z = zbuf[0:wi, h, b * P:(b + 1) * P]
                    if how.startswith("add"):
                        last = pe.transpose(prod[h][:, b * wo:(b + 1) * wo], z, ident[0:wi, 0:wo])
                        continue
                    last = pe.matmul(prod[h][:, b * wo:(b + 1) * wo], z, w, start=True, stop=True)
                    if how == "attention":
                        last = pe.matmul(prod_w1[h][:, b * 64:(b + 1) * 64], z, l3_w[:, 128:192], start=True, stop=True)
                last.then_inc(z_used, 1)

            def turn_table(f, i, h):
                wo = STAGES[f][3]
                n = INIT_STAGES.index(f) * STEPS + i
                pe.wait_ge(finished, f * STEPS + i + 1)
                if not (isinstance(n, int) and n == 0):
                    pe.wait_ge(init_done, n)
                settle(pe)
                for b in range(SB):
                    last = pe.transpose(back[0:wo, b * P:(b + 1) * P], stage[:, h, b * wo:(b + 1) * wo], ident[:])
                last.then_inc(back_ready, 1)

            def node_stage(f):
                init = f in INIT_STAGES
                if f in NORM_STAGES:
                    turn_nodes(f, 0, 0)
                for j in turns(pe, STEPS // 2, tail=1):
                    for h in range(2):
                        i = 2 * j + h
                        if f in NORM_STAGES and not (isinstance(i, int) and i == STEPS - 1):
                            turn_nodes(f, i + 1, 1 - h)
                        if STAGES[f][1] != "norm_only":
                            multiply(f, i, h)
                        if init and not at_start(i):
                            turn_table(f, i - 1, 1 - h)
                if init:
                    turn_table(f, STEPS - 1, 1)

            def sum_chunk(q, t, k):
                n = PASS0(q) + t * K + k
                w = PASS_WIDTH[q]
                pe.wait_ge(onehot_ready, n + 1)
                pe.wait_ge(gathered_s[k], 16 * (TURN0(q) + t + 1))
                if not (isinstance(n, int) and n < 4):
                    pe.wait_ge(added, n - 3)
                pe.matmul(window[k % 4][0:w], gathered[:, k, 0:w], onehot[:, k % 4, :], start=True, stop=True)\
                    .then_inc(summed, 1)

            def sum_pass(q, f, beside=None):
                pe.wait_ge(z_ready, (f + 1) * STEPS)
                for t in turns(pe, TURNS):
                    for k in range(K):
                        sum_chunk(q, t, k)
                        if beside:
                            beside(t, k)

            def edge_pass(q, f):
                pe.wait_ge(z_ready, (f + 1) * STEPS)
                pe.wait_ge(finished, (f + 1) * STEPS)
                for j in turns(pe, TURNS // 2, peel=q == EDGE_PASSES[0]):
                    for par in range(2):
                        for k in range(K):
                            sum_chunk(q, 2 * j + par, k)
                            edge_step(q, par, 2 * j + par, k)
                pe.wait_ge(e_dve, EDGE_TURN0(q + 1))

            def edge_step(q, par, t, k):
                g = EDGE_TURN0(q) + t
                if k == 1:
                    if par == 0:
                        pe.wait_ge(e_loaded, 8 * g + 16)
                        w, x = mlp[0:6, 0, :], e_in
                    else:
                        pe.wait_ge(e_act, 3 * g)
                        w, x = mlp[:, 1, :], e_z
                    if not (isinstance(g, int) and g == 0):
                        pe.wait_ge(e_dve, g)
                    pe.matmul(e_prod, w, x, start=True, stop=True).then_inc(e_mm, 1)
                elif k == 5:
                    pe.wait_ge(e_act, 3 * g + 1)
                    pe.matmul(e_var, blk[:], e_sq, start=True, stop=True).then_inc(e_mm, 1)

            def count_step(q):
                def step(t, k):
                    if k == 3:
                        pe.wait_ge(hist_ready, (q - 1) * TURNS + t + 1)
                        for x in range(K):
                            last = pe.matmul(hist, hist_lo[:, x, :], hist_hi[:, x, :], start=False, stop=False)
                        last.then_inc(hist_used, 1)
                return step

            node_stage(0)
            pe.wait_ge(moved, 32)
            sum_pass(0, 0)
            node_stage(1)
            for q in (1, 2):
                if q == 2:
                    pe.wait_ge(deg_sum, 1)
                pe.wait_ge(finished, (q + 1) * STEPS)
                pe.matmul(hist, zeros_b[:], zeros_b[:, 0:BLOCKS], start=True, stop=False)
                sum_pass(q, q, count_step(q))
                pe.matmul(hist, zeros_b[:], zeros_b[:, 0:BLOCKS], start=False, stop=True).then_inc(hist_closed, 1)
                node_stage(q + 1)
            node_stage(4)
            for q, f in ((3, 5), (4, 6), (5, 7)):
                edge_pass(q, f - 1)
                node_stage(f)
            node_stage(8)
            edge_pass(6, 8)
            node_stage(9)
            node_stage(10)

            pe.wait_ge(finished, 11 * STEPS)
            pe.wait_ge(z_ready, 11 * STEPS)
            pe.wait_ge(star_ready, 1)
            pe.matmul(star, zeros_b[:, 0:64], zeros_b[:, 0:1], start=True, stop=False)

            def collect(c, x, k):
                j, s = k // 2, k % 2
                n = PASS0(7) + c * GROUP + k
                if k == 0:
                    pe.wait_ge(rows_ready, c + 1)
                if s == 1:
                    pe.matmul(star, m_rows[x][:, j, :], star_sel[:, bass.ds(c * 4 + j, 1)], start=False, stop=False)
                if k % 4 == 0:
                    pe.wait_ge(ends_ready, 2 * c + 1 + k // 4)
                pe.wait_ge(added, n - 1)
                pe.matmul(window3[k % 2], os_rows[x][:, j, s, :], ends[k // 4][:, k % 4, :], start=True, stop=True)\
                    .then_inc(summed, 1)

            def logits(c, t, h, between, halfway=None):
                pe.wait_ge(in3[h], 16 * IN3 * (t + 1))
                if not (isinstance(c, int) and c < 2):
                    pe.wait_ge(excess_ready, c - 1)
                pe.matmul(logit[h], ident[:], dt_in[:, h, :], start=True, stop=False, skip_group_check=True)
                for s in range(2):
                    for j in range(4):
                        k = 2 * j + s
                        to = logit[h][s * D:(s + 1) * D, j * P:(j + 1) * P]
                        pe.wait_ge(gathered_s[h * GROUP + k], 16 * (TURN0(7) + t + 1))
                        pe.matmul(to, gathered[:, h * GROUP + k, 0:64], ident[:], start=False, stop=False,
                                  skip_group_check=True)
                        if j == 3:
                            between()
                if halfway:
                    halfway()
                for s in range(2):
                    pe.wait_ge(spread_ready, 2 * c + s + 1)
                    for j in range(4):
                        k = 2 * j + s
                        to = logit[h][s * D:(s + 1) * D, j * P:(j + 1) * P]
                        last = pe.matmul(to, w1_win[:, h * GROUP + k, :], spread[:, 4 * s + j, :], start=False,
                                         stop=k == GROUP - 1, skip_group_check=True)
                        if k == GROUP - 1:
                            last.then_inc(logits_ready, 1)
                        elif j == 3 or (s, j) == (0, 1):
                            between()

            def turn_back(c, h, between):
                pe.wait_ge(scans_done, c + 1)
                if not at_start(c):
                    pe.wait_ge(rows_ready, c)
                settle(pe)
                for j in range(4):
                    pe.transpose(o_back[:, j * P:(j + 1) * P], oo[:, h, j * P:(j + 1) * P], ident[:])
                between()
                for j in range(4):
                    last = pe.transpose(s_back[:, j * P:(j + 1) * P], ss[:, h, j * P:(j + 1) * P], ident[:])
                last.then_inc(turned_back, 1)
                between()

            def turn_maxima(c, h):
                pe.wait_ge(o_copied, c + 1)
                settle(pe)
                for j in range(4):
                    last = pe.transpose(m_back[:, j * P:(j + 1) * P], mm[:, h, 1 + j * P:1 + (j + 1) * P], ident[:])
                last.then_inc(m_turned, 1)

            def values(c, h, between):
                between()
                if not at_start(c):
                    pe.wait_ge(pw_ready, c)
                pe.matmul(value, ident[:], dt_in[:, h, :], start=True, stop=False, skip_group_check=True)
                for k in range(GROUP):
                    j, s = k // 2, k % 2
                    last = pe.matmul(value[s * D:(s + 1) * D, j * P:(j + 1) * P], gathered[:, h * GROUP + k, 64:128],
                                     ident[:], start=False, stop=k == GROUP - 1, skip_group_check=True)
                    if k == GROUP // 2 - 1:
                        between()
                last.then_inc(values_ready, 1)

            logits(0, 0, 0, lambda: None)
            for t in turns(pe, TURNS, tail=1):
                for h in range(2):
                    c = 2 * t + h
                    collected = [0]

                    def between():
                        if not at_start(t) and collected[0] < GROUP:
                            collect(c - 2, h, collected[0])
                            collected[0] += 1

                    values(c, h, between)
                    if not at_start(c):
                        turn_back(c - 1, 1 - h, between)
                    if not (isinstance(c, int) and c == GROUPS - 1):
                        logits(c + 1, t + h, 1 - h, between,
                               None if at_start(c) else lambda: turn_maxima(c - 1, 1 - h))
                    else:
                        turn_maxima(c - 1, 1 - h)
                    while not at_start(t) and collected[0] < GROUP:
                        between()
            for k in range(GROUP):
                collect(GROUPS - 2, 0, k)
            turn_back(GROUPS - 1, 1, lambda: None)
            turn_maxima(GROUPS - 1, 1)
            for k in range(GROUP):
                collect(GROUPS - 1, 1, k)
            pe.matmul(star, zeros_b[:, 0:64], zeros_b[:, 0:1], start=False, stop=True).then_inc(fix_pe, 1)
            pe.wait_ge(fix_dve, 2)
            pe.wait_ge(fix_act, 1)
            pe.wait_ge(rows_ready, GROUPS)
            pe.matmul(fix_ps[:, 0:2], spread[0:D, 0, :], fix[0:D, 2:4], start=True, stop=True)
            pe.matmul(fix_ps[:, 2:3], ident[0:D, :], oo[0:D, 1, GCOLS - 1:GCOLS], start=True, stop=False)
            pe.matmul(fix_ps[:, 2:3], spread[0:D, 1, :], ss[0:D, 1, GCOLS - 1:GCOLS], start=False, stop=True)\
                .then_inc(fix_pe, 1)
            node_stage(11)


def _columns(v, fill):
    import numpy as np
    v = np.concatenate([v, np.full(EDGES - N_EDGES, fill, v.dtype)]).reshape(2, CHUNKS // 2, P)
    return np.ascontiguousarray(v.transpose(2, 1, 0).reshape(P, CHUNKS))


def kernel(**inputs):
    import numpy as np
    import concourse.bacc as bacc
    from concourse.bass_utils import run_bass_kernel_spmd

    i = {k: np.asarray(v) for k, v in inputs.items()}
    src = _columns(i["src"], N_NODES)
    dst = _columns(i["dst"], N_NODES)
    after = np.concatenate([i["dst"][1:], np.full(1, N_NODES, i["dst"].dtype)])
    row = np.concatenate([i["dst"], np.full(EDGES - N_EDGES, N_NODES, i["dst"].dtype)]).reshape(2, HALF)
    attr = np.concatenate([i["edge_attr_3"], np.zeros((EDGES - N_EDGES, 3), i["edge_attr_3"].dtype)])
    arrays = {
        "x": np.concatenate([i["x"], np.zeros((NP - N_NODES, D), i["x"].dtype)]),
        "src": np.concatenate([src, src[:, :K]], axis=1),
        "dst": dst,
        "dst_next": _columns(after, N_NODES),
        "ew": _columns(i["edge_weight"], 0.0),
        "base": dst[0:1, :],
        "dst_rows": np.concatenate([np.full((2, 1), -1, row.dtype), row], axis=1),
        "edge_attr": attr.reshape(2, HALF, 3).transpose(0, 2, 1).reshape(6, HALF),
        "l0_w": i["L0_gnn_W"], "l0_b": i["L0_gnn_b"].T, "l0_gamma": i["L0_gnn_bn_gamma"].T,
        "l0_beta": i["L0_gnn_bn_beta"].T, "l0_prelu": i["L0_gnn_prelu_a"],
        "l1_w1": i["L1_gnn_W1"].T, "l1_w2": i["L1_gnn_W2"].T, "l1_w3": i["L1_gnn_W3"].T,
        "l1_b": np.concatenate([i["L1_gnn_b1"], i["L1_gnn_b2"], i["L1_gnn_b3"]]),
        "l3_w1": i["L3_gnn_W1"], "l3_w2": i["L3_gnn_W2"], "l3_w3": i["L3_gnn_W3"],
        "wd1": i["L3_gnn_Wd1"], "wd2": i["L3_gnn_Wd2"],
        "mlp_b": np.stack([np.stack([i["L3_gnn_" + n + str(layer)] for n in ("bd", "g", "b")], axis=1)
                           for layer in (1, 2)], axis=1),
    }
    arrays = {"in_" + k: np.ascontiguousarray(v) for k, v in arrays.items()}
    nc = bacc.Bacc("TRN2", target_bir_lowering=False, num_devices=1)
    args = {k[3:]: nc.dram_tensor(k, v.shape, mybir.dt.from_np(v.dtype), kind="ExternalInput").ap()
            for k, v in arrays.items()}
    args["out"] = nc.dram_tensor("out", [N_NODES, D], F32, kind="ExternalOutput").ap()
    build(nc, args)
    r = run_bass_kernel_spmd(nc, [arrays], core_ids=[0])
    return r.results[0]["out"]
```
